# Optimizing a Trainium2 kernel written in Bass

```python
import numpy as np
import jax
import jax.numpy as jnp

def _softmax(x, axis=-1):
    return jax.nn.softmax(x, axis=axis)
def _gelu(x):
    return jax.nn.gelu(x, approximate=True)
def _silu(x):
    return jax.nn.silu(x)
def _sigmoid(x):
    return jax.nn.sigmoid(x)
def _layernorm(x, axis=-1, eps=1e-5):
    m = jnp.mean(x, axis=axis, keepdims=True)
    v = jnp.var(x, axis=axis, keepdims=True)
    return (x - m) / jnp.sqrt(v + eps)
def _scatter_add(tgt, idx, src, axis=0):
    return tgt.at[idx].add(src)
def _segment_sum(src, seg, n):
    return jax.ops.segment_sum(src, seg, n)

kernel_name = 'mk_conv_seq_d2_conv_nchw16_966c42'

def setup_inputs(seed: int = 0):
    np.random.seed(seed)
    _w = jnp.asarray
    def _rec_inputs():
        import jax
        import jax.numpy as jnp
        _gk = jax.random.key(seed)
        x = -0.000125 + 0.9999 * jax.random.normal(jax.random.fold_in(_gk, 1), (32, 16, 256, 256), jnp.float32)
        return x
    x = _rec_inputs()
    def _L0_conv_setup():
        import jax, jax.numpy as jnp
        import numpy as np
        from jax import lax
        SOBEL_X = jnp.array([[-1.0, 0.0, 1.0], [-2.0, 0.0, 2.0], [-1.0, 0.0, 1.0]], dtype=jnp.float32)
        ALIVE_THRESH = 0.1

        def _depthwise3x3(x, kern2d):
            c = x.shape[1]
            kern = jnp.broadcast_to(kern2d.astype(x.dtype), (c, 1, 3, 3))
            return lax.conv_general_dilated(x, kern, window_strides=(1, 1), padding='SAME', dimension_numbers=('NCHW', 'OIHW', 'NCHW'), feature_group_count=c)
        key = jax.random.key(seed)
        k0, k1, k2, k3 = jax.random.split(key, 4)
        B, C, H, W = (32, 16, 256, 256)
        HID = 128
        grid = jax.random.normal(k0, (B, C, H, W), dtype=jnp.float32)
        rand_u = jax.random.uniform(k1, (H, W), dtype=jnp.float32)
        W1 = jax.random.normal(k2, (HID, 3 * C), dtype=jnp.float32) * 0.05
        b1 = jnp.zeros((HID,), dtype=jnp.float32)
        W2 = jax.random.normal(k3, (C, HID), dtype=jnp.float32) * 0.05
        b2 = jnp.zeros((C,), dtype=jnp.float32)
        return {'grid': grid, 'rand_u': rand_u, 'W1': W1, 'b1': b1, 'W2': W2, 'b2': b2}
    _L0_conv_all = _L0_conv_setup()
    _L0_conv_in = {k: v for k, v in _L0_conv_all.items() if k in ('rand_u', 'W1', 'b1', 'W2', 'b2', )}
    del _L0_conv_all

    def _L1_conv_setup():
        import jax, jax.numpy as jnp
        import numpy as np

        def _conv2d_same(x, w, b):
            y = jax.lax.conv_general_dilated(x, w, window_strides=(1, 1), padding=((1, 1), (1, 1)), dimension_numbers=('NCHW', 'OIHW', 'NCHW'))
            return y + b[None, :, None, None]
        key = jax.random.key(seed)
        ks = jax.random.split(key, 5)
        B, C, H, W = (16, 16, 512, 512)
        K = 3
        bound = float(np.sqrt(1.0 / (C * K * K)))
        x = jax.random.normal(ks[0], (B, C, H, W), dtype=jnp.float32)
        w1 = jax.random.uniform(ks[1], (C, C, K, K), minval=-bound, maxval=bound, dtype=jnp.float32)
        b1 = jax.random.uniform(ks[2], (C,), minval=-bound, maxval=bound, dtype=jnp.float32)
        w2 = jax.random.uniform(ks[3], (C, C, K, K), minval=-bound, maxval=bound, dtype=jnp.float32)
        b2 = jax.random.uniform(ks[4], (C,), minval=-bound, maxval=bound, dtype=jnp.float32)
        return {'x': x, 'w1': w1, 'b1': b1, 'w2': w2, 'b2': b2}
    _L1_conv_all = _L1_conv_setup()
    _L1_conv_in = {k: v for k, v in _L1_conv_all.items() if k in ('w1', 'b1', 'w2', 'b2', )}
    del _L1_conv_all

    return {
        "x": x,
        "L0_conv_rand_u": _L0_conv_in["rand_u"],
        "L0_conv_W1": _L0_conv_in["W1"],
        "L0_conv_b1": _L0_conv_in["b1"],
        "L0_conv_W2": _L0_conv_in["W2"],
        "L0_conv_b2": _L0_conv_in["b2"],
        "L1_conv_w1": _L1_conv_in["w1"],
        "L1_conv_b1": _L1_conv_in["b1"],
        "L1_conv_w2": _L1_conv_in["w2"],
        "L1_conv_b2": _L1_conv_in["b2"],
    }

def reference(x, L0_conv_rand_u, L0_conv_W1, L0_conv_b1, L0_conv_W2, L0_conv_b2, L1_conv_w1, L1_conv_b1, L1_conv_w2, L1_conv_b2):
    import jax
    import jax.numpy as jnp
    def _L0_conv_ref(grid, rand_u, W1, b1, W2, b2):
        import jax, jax.numpy as jnp
        import numpy as np
        from jax import lax
        SOBEL_X = jnp.array([[-1.0, 0.0, 1.0], [-2.0, 0.0, 2.0], [-1.0, 0.0, 1.0]], dtype=jnp.float32)
        ALIVE_THRESH = 0.1

        def _depthwise3x3(x, kern2d):
            c = x.shape[1]
            kern = jnp.broadcast_to(kern2d.astype(x.dtype), (c, 1, 3, 3))
            return lax.conv_general_dilated(x, kern, window_strides=(1, 1), padding='SAME', dimension_numbers=('NCHW', 'OIHW', 'NCHW'), feature_group_count=c)
        sx = _depthwise3x3(grid, SOBEL_X)
        sy = _depthwise3x3(grid, SOBEL_X.T)
        p = jnp.concatenate([sx, sy, grid], axis=1)
        h = jax.nn.relu(jnp.einsum('bchw,oc->bohw', p, W1) + b1[None, :, None, None])
        delta = jnp.einsum('bchw,oc->bohw', h, W2) + b2[None, :, None, None]
        upd_mask = (rand_u < 0.5).astype(grid.dtype)
        x = grid + delta * upd_mask[None, None, :, :]
        alpha = lax.reduce_window(x[:, 3, :, :], -jnp.inf, lax.max, window_dimensions=(1, 3, 3), window_strides=(1, 1, 1), padding='SAME')
        alive = (alpha > ALIVE_THRESH).astype(x.dtype)
        return x * alive[:, None, :, :]

    def _L1_conv_ref(x, w1, b1, w2, b2):
        import jax, jax.numpy as jnp
        import numpy as np

        def _conv2d_same(x, w, b):
            y = jax.lax.conv_general_dilated(x, w, window_strides=(1, 1), padding=((1, 1), (1, 1)), dimension_numbers=('NCHW', 'OIHW', 'NCHW'))
            return y + b[None, :, None, None]
        out = _conv2d_same(x, w1, b1)
        out = jax.nn.relu(out)
        out = _conv2d_same(out, w2, b2)
        return out + x

    def _gn(v, G=8, eps=1e-5):
        B_, C_, H_, W_ = v.shape
        g = v.reshape(B_, G, C_ // G, H_, W_)
        m = jnp.mean(g, axis=(2, 3, 4), keepdims=True)
        s = jnp.var(g, axis=(2, 3, 4), keepdims=True)
        return ((g - m) / jnp.sqrt(s + eps)).reshape(v.shape)

    def _ln_c(v, eps=1e-6):
        m = jnp.mean(v, axis=1, keepdims=True)
        s = jnp.var(v, axis=1, keepdims=True)
        return (v - m) / jnp.sqrt(s + eps)

    def _ln_t(v, eps=1e-5):
        m = jnp.mean(v, axis=-1, keepdims=True)
        s = jnp.var(v, axis=-1, keepdims=True)
        return (v - m) / jnp.sqrt(s + eps)

    def _to_tokens(v):
        B_, C_, H_, W_ = v.shape
        return v.reshape(B_, C_, H_ * W_).transpose(0, 2, 1)
    def _from_tokens(t, like):
        B_, C_, H_, W_ = like.shape
        return t.transpose(0, 2, 1).reshape(B_, C_, H_, W_)

    x = _L0_conv_ref(x, L0_conv_rand_u, L0_conv_W1, L0_conv_b1, L0_conv_W2, L0_conv_b2)
    x = _L1_conv_ref(x, L1_conv_w1, L1_conv_b1, L1_conv_w2, L1_conv_b2)
    return x


_drawn_inputs = setup_inputs


def setup_inputs(seed=0):
    import zlib

    import numpy as np

    out = dict(_drawn_inputs(seed))
    spreads = {'L0_conv_b1': (0.0, 0.1), 'L0_conv_b2': (0.0, 0.1)}
    factors = {'L1_conv_b1': 3.337}
    for name, (base, spread) in spreads.items():
        noise = np.random.default_rng([zlib.crc32(name.encode()), seed]).standard_normal(out[name].shape)
        drawn = base * np.exp(spread * noise) if base else spread * noise
        out[name] = jnp.asarray(drawn.astype(out[name].dtype))
    for name, factor in factors.items():
        out[name] = (out[name] * factor).astype(out[name].dtype)
    return out
```

```python
from contextlib import ExitStack

import numpy as np

import concourse.bass as bass
from concourse import mybir

B, C, H, W = 32, 16, 256, 256
HID = 128
ROWS = 8
TILES = H // ROWS
PAIRS = TILES // 2
BLOCKS = PAIRS // 2
STRIP = 4
WP = W + 2
KINDS = 3
PARTS = 2 * KINDS
KROWS = PARTS * C
NPAIR = B * PAIRS
NBLOCK = B * BLOCKS
N = 2 * W
ALPHA = 3
XRING, ORING = 8, 4
CHUNKS = 4

LAG_XP = 1
LAG_POOL = 2
LAG_ALIVE = 3
LAG_C1 = 4
LAG_C2 = 5

BI_HID, BI_DELTA, BI_C1, BI_C1_TOP, BI_C1_LAST, BI_C2 = range(6)


def build_program(nc, xs_d, xl_d, ru_d, wa_d, w2_d, g1_d, g1v_d, g2_d, bias_d, out_d):
    f32, f32r, bf16 = mybir.dt.float32, mybir.dt.float32r, mybir.dt.bfloat16
    ALU = mybir.AluOpType
    ACT = mybir.ActivationFunctionType

    alpha_d = nc.dram_tensor("alpha_scratch", (B, H + 2, W), f32).ap()
    mask_d = nc.dram_tensor("mask_scratch", (B, H, W), bf16).ap()

    ctx = ExitStack()
    with ctx:
        def sb(name, shape, dt=f32):
            return ctx.enter_context(nc.sbuf_tensor(name, shape, dt))

        def pb(name, shape):
            return ctx.enter_context(nc.psum_tensor(name, shape, f32))

        def sem(name):
            return ctx.enter_context(nc.semaphore(name))

        wa = sb("wa", [KROWS, HID])
        wa_hi = sb("wa_hi", [KROWS, HID], f32r)
        wa_lo = sb("wa_lo", [KROWS, HID], f32r)
        w2 = sb("w2", [HID, 2, 32])
        g1 = sb("g1", [128, 3, 3, 32])
        g1v = sb("g1v", [128, 2, 3, 32])
        g2 = sb("g2", [128, 3, 3, 32])
        bias = sb("bias", [128, 6])
        upd = sb("upd", [128, TILES, W], bf16)
        xs = sb("xs", [128, 2, STRIP + 2, WP])
        diff = sb("diff", [128, STRIP + 2, WP])
        duo = sb("duo", [128, STRIP + 1, W + 1])
        sx = sb("sx", [128, STRIP, W])
        sy = sb("sy", [128, STRIP, W])
        parts = sb("parts", [128, 2, PARTS, STRIP * W], f32r)
        perc = sb("perc", [KROWS, 2, 2, ROWS, W], f32r)
        hid = sb("hid", [HID, ROWS, N])
        delta = sb("delta", [128, N])
        x = sb("x", [128, XRING, 2, WP])
        nb = sb("nb", [16, 2, 3, WP])
        m1 = sb("m1", [16, WP])
        m2 = sb("m2", [16, WP])
        m3 = sb("m3", [16, W])
        m4 = sb("m4", [16, W])
        alive = sb("alive", [16, 2, W], bf16)
        alive_b = sb("alive_b", [128, 2, 2, W], bf16)
        st0 = sb("st0", [128, WP])
        st1 = sb("st1", [128, 2, 2, WP])
        st2 = sb("st2", [128, 2, 2, WP])
        o1 = sb("o1", [128, ORING, 2, WP])
        o1_top = sb("o1_top", [128, WP])
        y = sb("y", [128, 2, N])

        ps_hid = [pb(f"ps_hid{n}", [HID, 2, N]) for n in range(2)]
        ps_delta = pb("ps_delta", [128, N])
        ps_c1 = pb("ps_c1", [128, N])
        ps_c2 = pb("ps_c2", [128, N])
        ps_top = pb("ps_top", [128, N])

        s_const = sem("s_const")
        s_ru = sem("s_ru")
        s_upd = sem("s_upd")
        s_zero = sem("s_zero")
        s_wsplit = sem("s_wsplit")
        s_alpha0 = sem("s_alpha0")
        s_xs = [sem(f"s_xs{n}") for n in range(2)]
        s_xl = [sem(f"s_xl{n}") for n in range(2)]
        s_dx = sem("s_dx")
        s_tx = sem("s_tx")
        s_sx = sem("s_sx")
        s_dy = sem("s_dy")
        s_ty = sem("s_ty")
        s_sy = sem("s_sy")
        s_hi = [sem(f"s_hi{n}") for n in range(KINDS)]
        s_lo = [sem(f"s_lo{n}") for n in range(KINDS)]
        s_perc = [sem(f"s_perc{n}") for n in range(2)]
        s_hmm = sem("s_hmm")
        s_hev = sem("s_hev")
        s_dmm = sem("s_dmm")
        s_dev = sem("s_dev")
        s_x1 = sem("s_x1")
        s_aw = sem("s_aw")
        s_nb = [sem(f"s_nb{n}") for n in range(2)]
        s_m1, s_m2, s_m3, s_m4 = (sem(f"s_m{n}") for n in range(1, 5))
        s_alive = sem("s_alive")
        s_mw = sem("s_mw")
        s_mb = [sem(f"s_mb{n}") for n in range(2)]
        s_x2 = sem("s_x2")
        s_st0 = sem("s_st0")
        s_st1 = [sem(f"s_st1_{n}") for n in range(2)]
        s_c1 = sem("s_c1")
        s_top = sem("s_top")
        s_topev = sem("s_topev")
        s_o1 = sem("s_o1")
        s_st2 = [sem(f"s_st2_{n}") for n in range(2)]
        s_c2 = sem("s_c2")
        s_y = sem("s_y")
        s_out = [sem(f"s_out{n}") for n in range(2)]
        s_sp_gate = sem("s_sp_gate")

        block = ctx.enter_context(nc.Block())

        def val(i, per_image, offset):
            return i * per_image + offset

        def after(eng, semaphore, i, per_image, offset):
            v = val(i, per_image, offset)
            if isinstance(i, int) and v <= 0:
                return
            eng.wait_ge(semaphore, v)

        def gated(eng, gate, semaphore, i, per_image, offset):
            v = val(i, per_image, offset)
            if isinstance(i, int):
                if v > 0:
                    eng.wait_ge(semaphore, v)
                return
            eng.wait_ge(semaphore, v)
            eng.sem_inc(gate, 1)

        def there(i, q, of=NPAIR, per_image=PAIRS):
            return not isinstance(i, int) or 0 <= i * per_image + q < of

        def walk(eng, step):
            for s in range(-6, PAIRS):
                step(0, s)
            with eng.Fori(1, B - 1) as i:
                for j in range(PAIRS):
                    step(i, j)
            for j in range(PAIRS + LAG_C2 + 1):
                step(B - 1, j)

        @block.sync
        def _(sp):
            for dst, src in ((wa, wa_d), (w2, w2_d), (g1, g1_d), (g1v, g1v_d), (g2, g2_d), (bias, bias_d)):
                sp.dma_start(dst[:], src).then_inc(s_const, 16)
            half = TILES // 2 * W
            for n in range(2):
                if n:
                    sp.wait_ge(s_upd, n)
                sp.dma_start(
                    hid[:].rearrange("p r n -> p (r n)"),
                    ru_d[:, n * half:(n + 1) * half].unsqueeze(1).to_broadcast([ROWS, C, half]),
                ).then_inc(s_ru, 16)
            sp.wait_ge(s_zero, 1)
            sp.dma_start(alpha_d[:, 0:H + 2:H + 1, :], st1[0:B, 0, :, 0:W]).then_inc(s_alpha0, 16)

            def load_block(i, b):
                if not there(i, b, NBLOCK, BLOCKS):
                    return
                gated(sp, s_sp_gate, s_dy, i, BLOCKS, b - 1)
                gated(sp, s_sp_gate, s_lo[2], i, BLOCKS, b - 1)
                sp.dma_start(xs[:, b % 2].rearrange("p r w -> p (r w)"),
                             xs_d[val(i, BLOCKS, b)]).then_inc(s_xs[b % 2], 16)

            def load_pair(i, q):
                if not there(i, q):
                    return
                gated(sp, s_sp_gate, s_y, i, PAIRS, q - XRING + 1)
                sp.dma_start(x[:, q % XRING, :, 1:1 + W],
                             xl_d[val(i, PAIRS, q)].rearrange("p (t w) -> p t w", t=2)).then_inc(s_xl[q % 2], 16)

            def gather_perception(i, q):
                if not there(i, q):
                    return
                b = q // 2
                for kind in range(KINDS):
                    gated(sp, s_sp_gate, s_lo[kind], i, BLOCKS, b + 1)
                gated(sp, s_sp_gate, s_hmm, i, CHUNKS * PAIRS, CHUNKS * (q - 1))
                for n in range(4):
                    g = 4 * (q % 2) + n
                    sp.dma_start(
                        perc[:, q % 2, n // 2, STRIP * (n % 2):STRIP * (n % 2 + 1), :].rearrange("k r w -> k (r w)").bitcast(f32),
                        parts[C * g:C * g + C, b % 2, :, :].bitcast(f32),
                    ).then_inc(s_perc[q % 2], 16)

            def write_alpha(i, q):
                if not there(i, q):
                    return
                gated(sp, s_sp_gate, s_x1, i, PAIRS, q + 1)
                img, j = i + q // PAIRS, q % PAIRS
                rows = alpha_d[img, 1 + 16 * j:1 + 16 * j + 16, :].rearrange("(t r) w -> r t w", t=2)
                sp.dma_start(rows, x[ALPHA::C, q % XRING, :, 1:1 + W]).then_inc(s_aw, 16)

            def load_neighbours(i, q):
                if not there(i, q):
                    return
                img, j = i + q // PAIRS, q % PAIRS
                below = 2 if j < PAIRS - 1 else 1
                gated(sp, s_sp_gate, s_aw, i, 16 * PAIRS, 16 * (q + below))
                gated(sp, s_sp_gate, s_m2, i, PAIRS, q - 1)
                src = alpha_d[img, 16 * j:16 * j + 16, :]
                src = bass.AP(tensor=src.tensor, offset=src.offset, ap=[[W, 16], [W, 3], [1, W]])
                sp.dma_start(nb[:, q % 2, :, 1:1 + W], src).then_inc(s_nb[q % 2], 16)

            def write_mask(i, q):
                if not there(i, q):
                    return
                gated(sp, s_sp_gate, s_alive, i, PAIRS, q + 1)
                img, j = i + q // PAIRS, q % PAIRS
                sp.dma_start(mask_d[img, 16 * j:16 * j + 16, :], alive[:, q % 2, :]).then_inc(s_mw, 16)

            def load_mask(i, q):
                if not there(i, q):
                    return
                img, j = i + q // PAIRS, q % PAIRS
                gated(sp, s_sp_gate, s_mw, i, 16 * PAIRS, 16 * (q + 1))
                gated(sp, s_sp_gate, s_x2, i, PAIRS, q - 1)
                src = mask_d[img, 16 * j:16 * j + 16, :].rearrange("(t r) w -> r t w", t=2)
                for t in range(2):
                    sp.dma_start(alive_b[:, q % 2, t, :],
                                 src[:, t, :].unsqueeze(1).to_broadcast([ROWS, C, W])).then_inc(s_mb[q % 2], 16)

            def gather_st1(i, q):
                if not there(i, q):
                    return
                j, slot = q % PAIRS, q % XRING
                last = j == PAIRS - 1
                gated(sp, s_sp_gate, s_x2, i, PAIRS, q + (1 if last else 2))
                gated(sp, s_sp_gate, s_c1, i, PAIRS, q - 1)
                if j == 0:
                    sp.dma_start(st0[32:64, :], x[0:32, slot, 0, :]).then_inc(s_st0, 16)
                sp.dma_start(st1[0:32, q % 2], x[96:128, slot]).then_inc(s_st1[q % 2], 16)
                sp.dma_start(st1[32:64, q % 2, 0], x[0:32, slot, 1]).then_inc(s_st1[q % 2], 16)
                below = st0[0:32, :] if last else x[0:32, (slot + 1) % XRING, 0]
                sp.dma_start(st1[32:64, q % 2, 1], below).then_inc(s_st1[q % 2], 16)

            def gather_st2(i, q):
                if not there(i, q):
                    return
                j, slot = q % PAIRS, q % ORING
                gated(sp, s_sp_gate, s_o1, i, PAIRS, q + 1)
                gated(sp, s_sp_gate, s_c2, i, PAIRS, q - 1)
                if j == 0:
                    gated(sp, s_sp_gate, s_topev, i, 1, q // PAIRS + 1)
                above = o1_top[96:128, :] if j == 0 else o1[96:128, (slot - 1) % ORING, 1]
                sp.dma_start(st2[0:32, q % 2, 0], above).then_inc(s_st2[q % 2], 16)
                sp.dma_start(st2[0:32, q % 2, 1], o1[96:128, slot, 0]).then_inc(s_st2[q % 2], 16)
                sp.dma_start(st2[32:64, q % 2], o1[0:32, slot]).then_inc(s_st2[q % 2], 16)

            def store(i, q):
                if not there(i, q):
                    return
                gated(sp, s_sp_gate, s_y, i, PAIRS, q + 1)
                sp.dma_start(out_d[val(i, PAIRS, q)], y[:, q % 2, :]).then_inc(s_out[q % 2], 16)

            def step(i, j):
                if j % 2 == 0:
                    load_block(i, (j + 6) // 2)
                gather_perception(i, j + 1)
                write_alpha(i, j - LAG_XP)
                load_pair(i, j + 2)
                gather_st1(i, j - LAG_C1)
                load_neighbours(i, j - LAG_POOL)
                store(i, j - LAG_C2)
                write_mask(i, j - LAG_POOL)
                load_mask(i, j - LAG_POOL)
                gather_st2(i, j - LAG_C1)

            sp.wait_ge(s_zero, 2)
            sp.wait_ge(s_alpha0, 16)
            walk(sp, step)
            for n in range(2):
                sp.wait_ge(s_out[n], 16 * NPAIR // 2)

        @block.gpsimd
        def _(pool):
            def sobel_x(i, b):
                if not there(i, b, NBLOCK, BLOCKS):
                    return
                src = xs[:, b % 2]
                after(pool, s_xs[b % 2], i, 16 * BLOCKS // 2, 16 * (b // 2 + 1))
                after(pool, s_ty, i, BLOCKS, b)
                pool.tensor_tensor(diff[:, :, 0:W], src[:, :, 2:WP], src[:, :, 0:W], ALU.subtract).then_inc(s_dx, 1)
                after(pool, s_dx, i, BLOCKS, b + 1)
                after(pool, s_sy, i, BLOCKS, b)
                pool.tensor_tensor(duo[:, :, 0:W], diff[:, 0:STRIP + 1, 0:W], diff[:, 1:STRIP + 2, 0:W],
                                   ALU.add).then_inc(s_tx, 1)
                after(pool, s_tx, i, BLOCKS, b + 1)
                after(pool, s_lo[0], i, BLOCKS, b)
                pool.tensor_tensor(sx[:], duo[:, 0:STRIP, 0:W], duo[:, 1:STRIP + 1, 0:W], ALU.add).then_inc(s_sx, 1)

            def sobel_y(i, b):
                if not there(i, b, NBLOCK, BLOCKS):
                    return
                src = xs[:, b % 2]
                after(pool, s_tx, i, BLOCKS, b + 1)
                pool.tensor_tensor(diff[:, 0:STRIP, :], src[:, 2:STRIP + 2, :], src[:, 0:STRIP, :],
                                   ALU.subtract).then_inc(s_dy, 1)
                after(pool, s_dy, i, BLOCKS, b + 1)
                after(pool, s_sx, i, BLOCKS, b + 1)
                pool.tensor_tensor(duo[:, 0:STRIP, 0:W + 1], diff[:, 0:STRIP, 0:W + 1], diff[:, 0:STRIP, 1:WP],
                                   ALU.add).then_inc(s_ty, 1)
                after(pool, s_ty, i, BLOCKS, b + 1)
                after(pool, s_lo[1], i, BLOCKS, b)
                pool.tensor_tensor(sy[:], duo[:, 0:STRIP, 0:W], duo[:, 0:STRIP, 1:1 + W], ALU.add).then_inc(s_sy, 1)

            def step(i, j):
                if j % 2 == 0:
                    sobel_x(i, (j + 4) // 2)
                else:
                    sobel_y(i, (j + 3) // 2)

            walk(pool, step)

        @block.scalar
        def _(act):
            def hidden(i, q, m):
                if not there(i, q):
                    return
                after(act, s_hmm, i, CHUNKS * PAIRS, CHUNKS * q + m + 1)
                if m == 0:
                    after(act, s_dmm, i, PAIRS, q)
                nc.scalar.activation(hid[:, 2 * m:2 * m + 2, :], ps_hid[m % 2][:], ACT.Relu,
                                     bias=bias[:, BI_HID:BI_HID + 1]).then_inc(s_hev, 1)

            def conv1_out(i, q):
                if not there(i, q):
                    return
                j, slot = q % PAIRS, q % ORING
                if j == 0:
                    after(act, s_top, i, 1, q // PAIRS + 1)
                    nc.scalar.activation(o1_top[96:128, 1:1 + W], ps_top[96:128, 0:W], ACT.Relu,
                                         bias=bias[96:128, BI_C1_TOP:BI_C1_TOP + 1]).then_inc(s_topev, 1)
                after(act, s_c1, i, PAIRS, q + 1)
                after(act, s_c2, i, PAIRS, q - 2)
                src = ps_c1[:].rearrange("p (t w) -> p t w", t=2)
                if j < PAIRS - 1:
                    nc.scalar.activation(o1[:, slot, :, 1:1 + W], src, ACT.Relu,
                                         bias=bias[:, BI_C1:BI_C1 + 1]).then_inc(s_o1, 1)
                else:
                    nc.scalar.activation(o1[:, slot, 0, 1:1 + W], src[:, 0], ACT.Relu,
                                         bias=bias[:, BI_C1:BI_C1 + 1])
                    nc.scalar.activation(o1[:, slot, 1, 1:1 + W], src[:, 1], ACT.Relu,
                                         bias=bias[:, BI_C1_LAST:BI_C1_LAST + 1]).then_inc(s_o1, 1)

            def step(i, j):
                for m in range(CHUNKS):
                    hidden(i, j, m)
                conv1_out(i, j - LAG_C1)

            act.wait_ge(s_const, 96)
            act.wait_ge(s_upd, 2)
            act.wait_ge(s_zero, 2)
            walk(act, step)

        @block.vector
        def _(dve):
            dve.memset(st1[:], 0.0).then_inc(s_zero, 1)
            for buf in (x, o1, st2, nb, st0):
                dve.memset(buf[:], 0.0)
            dve.memset(o1_top[:], 0.0).then_inc(s_zero, 1)
            half = TILES // 2
            for n in range(2):
                dve.wait_ge(s_ru, 16 * (n + 1))
                dve.tensor_scalar(upd[:, n * half:(n + 1) * half, :].rearrange("p t w -> p (t w)"),
                                  hid[:].rearrange("p r n -> p (r n)"), 0.5, None, ALU.is_lt).then_inc(s_upd, 1)
            dve.wait_ge(s_const, 96)
            dve.tensor_copy(wa_hi[:], wa[:]).then_inc(s_wsplit, 1)
            dve.wait_ge(s_wsplit, 1)
            dve.tensor_tensor(wa_lo[:], wa[:], wa_hi[:].bitcast(f32), ALU.subtract).then_inc(s_wsplit, 1)
            dve.wait_ge(s_upd, 2)

            def source(kind, b):
                return (sx[:], sy[:], xs[:, b % 2, 1:1 + STRIP, 1:1 + W])[kind]

            def part(kind, b, dt=f32r):
                return parts[:, b % 2, kind, :].rearrange("p (r w) -> p r w", r=STRIP)

            def split_hi(i, b, kind):
                if not there(i, b, NBLOCK, BLOCKS):
                    return
                if kind == 0:
                    after(dve, s_sx, i, BLOCKS, b + 1)
                elif kind == 1:
                    after(dve, s_sy, i, BLOCKS, b + 1)
                else:
                    after(dve, s_xs[b % 2], i, 16 * BLOCKS // 2, 16 * (b // 2 + 1))
                    for n in range(2):
                        after(dve, s_perc[n], i, 64 * BLOCKS, 64 * (b - 1))
                dve.tensor_copy(part(kind, b), source(kind, b)).then_inc(s_hi[kind], 1)

            def split_lo(i, b, kind):
                if not there(i, b, NBLOCK, BLOCKS):
                    return
                after(dve, s_hi[kind], i, BLOCKS, b + 1)
                dve.tensor_tensor(part(KINDS + kind, b), source(kind, b), part(kind, b).bitcast(f32),
                                  ALU.subtract).then_inc(s_lo[kind], 1)

            def masked_delta(i, q):
                if not there(i, q):
                    return
                j = q % PAIRS
                after(dve, s_dmm, i, PAIRS, q + 1)
                after(dve, s_x1, i, PAIRS, q)
                dve.scalar_tensor_tensor(out=delta[:], in0=ps_delta[:], scalar=bias[:, BI_DELTA:BI_DELTA + 1],
                                         in1=upd[:, 2 * j:2 * j + 2, :].rearrange("p t w -> p (t w)"),
                                         op0=ALU.add, op1=ALU.mult).then_inc(s_dev, 1)

            def make_x1(i, q):
                if not there(i, q):
                    return
                after(dve, s_dev, i, PAIRS, q + 1)
                after(dve, s_xl[q % 2], i, 16 * PAIRS // 2, 16 * (q // 2 + 1))
                here = x[:, q % XRING, :, 1:1 + W]
                dve.tensor_tensor(here, here, delta[:].rearrange("p (t w) -> p t w", t=2), ALU.add).then_inc(s_x1, 1)

            def make_alive(i, q):
                if not there(i, q):
                    return
                rows = nb[:, q % 2]
                after(dve, s_nb[q % 2], i, 16 * PAIRS // 2, 16 * (q // 2 + 1))
                dve.tensor_tensor(m1[:], rows[:, 0], rows[:, 1], ALU.max).then_inc(s_m1, 1)
                after(dve, s_m1, i, PAIRS, q + 1)
                dve.tensor_tensor(m2[:], m1[:], rows[:, 2], ALU.max).then_inc(s_m2, 1)
                after(dve, s_m2, i, PAIRS, q + 1)
                dve.tensor_tensor(m3[:], m2[:, 0:W], m2[:, 1:1 + W], ALU.max).then_inc(s_m3, 1)
                after(dve, s_m3, i, PAIRS, q + 1)
                dve.tensor_tensor(m4[:], m3[:], m2[:, 2:WP], ALU.max).then_inc(s_m4, 1)
                after(dve, s_m4, i, PAIRS, q + 1)
                after(dve, s_mw, i, 16 * PAIRS, 16 * (q - 1))
                dve.tensor_scalar(alive[:, q % 2, :], m4[:], 0.1, None, ALU.is_gt).then_inc(s_alive, 1)

            def apply_alive(i, q):
                if not there(i, q):
                    return
                after(dve, s_mb[q % 2], i, 32 * PAIRS // 2, 32 * (q // 2 + 1))
                after(dve, s_aw, i, 16 * PAIRS, 16 * (q + 1))
                here = x[:, q % XRING, :, 1:1 + W]
                dve.tensor_tensor(here, here, alive_b[:, q % 2], ALU.mult).then_inc(s_x2, 1)

            def output(i, q):
                if not there(i, q):
                    return
                after(dve, s_c2, i, PAIRS, q + 1)
                after(dve, s_x2, i, PAIRS, q + 1)
                after(dve, s_out[q % 2], i, 16 * PAIRS // 2, 16 * (q // 2))
                dve.scalar_tensor_tensor(out=y[:, q % 2].rearrange("p (t w) -> p t w", t=2),
                                         in0=ps_c2[:].rearrange("p (t w) -> p t w", t=2),
                                         scalar=bias[:, BI_C2:BI_C2 + 1], in1=x[:, q % XRING, :, 1:1 + W],
                                         op0=ALU.add, op1=ALU.add).then_inc(s_y, 1)

            def step(i, j):
                odd = j % 2
                b = (j + 3) // 2 if odd else (j + 2) // 2
                masked_delta(i, j - LAG_XP)
                split_hi(i, b, 2 if odd else 1)
                make_x1(i, j - LAG_XP)
                apply_alive(i, j - LAG_ALIVE)
                if odd:
                    split_hi(i, b, 0)
                output(i, j - LAG_C2)
                split_lo(i, b, 2 if odd else 1)
                make_alive(i, j - LAG_POOL)
                if odd:
                    split_lo(i, b, 0)

            walk(dve, step)

        @block.tensor
        def _(pe):
            def hidden(i, q, m):
                if not there(i, q):
                    return
                if m == 0:
                    after(pe, s_perc[q % 2], i, 64 * PAIRS // 2, 64 * (q // 2 + 1))
                after(pe, s_hev, i, CHUNKS * PAIRS, CHUNKS * q + m - 1)
                for n in range(2):
                    r = 2 * m + n
                    rhs = perc[:, q % 2, :, r, :]
                    out = ps_hid[m % 2][:, n, :]
                    nc.tensor.matmul(out, wa_hi[:], rhs, start=True, stop=False)
                    last = nc.tensor.matmul(out, wa_lo[:], rhs, start=False, stop=True)
                last.then_inc(s_hmm, 1)

            def delta_products(i, q):
                if not there(i, q):
                    return
                after(pe, s_hev, i, CHUNKS * PAIRS, CHUNKS * (q + 1))
                after(pe, s_dev, i, PAIRS, q)
                for n in range(2):
                    for t in range(4):
                        last = nc.tensor.matmul(ps_delta[32 * t:32 * t + 32, :], w2[:, n, :], hid[:, 2 * t + n, :],
                                                start=(n == 0), stop=(n == 1))
                last.then_inc(s_dmm, 1)

            def conv1(i, q):
                if not there(i, q):
                    return
                j, slot = q % PAIRS, q % XRING
                after(pe, s_x2, i, PAIRS, q + 1)
                after(pe, s_o1, i, PAIRS, q)
                if j == 0:
                    after(pe, s_st0, i, 16, 16 * (q // PAIRS + 1))
                    after(pe, s_topev, i, 1, q // PAIRS)
                    for dx in range(3):
                        last = nc.tensor.matmul(ps_top[96:128, 0:W], g1v[:, 0, dx, :], st0[:, dx:dx + W],
                                                start=(dx == 0), stop=(dx == 2), tile_position=(0, 96))
                    last.then_inc(s_top, 1)
                after(pe, s_st1[q % 2], i, 48 * PAIRS // 2, 48 * (q // 2 + 1))
                halves = j == PAIRS - 1
                for dx in range(3):
                    for t in range(3):
                        last = nc.tensor.matmul(ps_c1[32 * t:32 * t + 32, :], g1[:, dx, t, :],
                                                x[:, slot, :, dx:dx + W], start=(dx == 0), stop=(dx == 2))
                    if not halves:
                        last = nc.tensor.matmul(ps_c1[96:128, :], g1[:, dx, 0, :], st1[:, q % 2, :, dx:dx + W],
                                                start=(dx == 0), stop=(dx == 2), tile_position=(0, 96))
                if halves:
                    for t in range(2):
                        for dx in range(3):
                            lhs = g1v[:, 1, dx, :] if t else g1[:, dx, 0, :]
                            last = nc.tensor.matmul(ps_c1[96:128, t * W:(t + 1) * W], lhs, st1[:, q % 2, t, dx:dx + W],
                                                    start=(dx == 0), stop=(dx == 2), tile_position=(0, 96))
                last.then_inc(s_c1, 1)

            def conv2(i, q):
                if not there(i, q):
                    return
                slot = q % ORING
                after(pe, s_o1, i, PAIRS, q + 1)
                after(pe, s_y, i, PAIRS, q)
                after(pe, s_st2[q % 2], i, 48 * PAIRS // 2, 48 * (q // 2 + 1))
                for dx in range(3):
                    for t in range(4):
                        rhs = o1[:, slot, :, dx:dx + W] if t else st2[:, q % 2, :, dx:dx + W]
                        last = nc.tensor.matmul(ps_c2[32 * t:32 * t + 32, :], g2[:, dx, max(t - 1, 0), :], rhs,
                                                start=(dx == 0), stop=(dx == 2), tile_position=(0, 32 * t))
                last.then_inc(s_c2, 1)

            def step(i, j):
                hidden(i, j, 0)
                hidden(i, j, 1)
                conv2(i, j - LAG_C2)
                hidden(i, j, 2)
                hidden(i, j, 3)
                conv1(i, j - LAG_C1)
                delta_products(i, j)

            pe.wait_ge(s_const, 96)
            pe.wait_ge(s_wsplit, 2)
            pe.wait_ge(s_zero, 2)
            walk(pe, step)


def band(w, place, first_rows=(0, 1)):
    out = np.zeros((128, 3, 32), w.dtype)
    for a in range(4):
        for r in first_rows:
            if 0 <= a - r <= 2:
                k = 32 * place + C * a
                out[k:k + C, :, C * r:C * r + C] = w[:, :, a - r, :].transpose(1, 2, 0)
    return out


def kernel(x, L0_conv_rand_u, L0_conv_W1, L0_conv_b1, L0_conv_W2, L0_conv_b2,
           L1_conv_w1, L1_conv_b1, L1_conv_w2, L1_conv_b2):
    import concourse.bacc as bacc
    from concourse.bass_utils import run_bass_kernel_spmd

    x = np.asarray(x)
    padded = np.zeros((B, C, H + 2, WP), x.dtype)
    padded[:, :, 1:-1, 1:-1] = x
    strips = np.lib.stride_tricks.sliding_window_view(padded, STRIP + 2, axis=2)[:, :, ::STRIP]
    strips = strips.reshape(B, C, BLOCKS, 8, WP, STRIP + 2).transpose(0, 2, 3, 1, 5, 4)
    xs = np.ascontiguousarray(strips).reshape(NBLOCK, 128, (STRIP + 2) * WP)
    xl = np.ascontiguousarray(x.reshape(B, C, PAIRS, 2, ROWS, W).transpose(0, 2, 4, 1, 3, 5)).reshape(NPAIR, 128, N)
    ru = np.asarray(L0_conv_rand_u)
    ru = np.ascontiguousarray(ru.reshape(TILES, ROWS, W).transpose(1, 0, 2)).reshape(ROWS, TILES * W)

    w1 = np.asarray(L0_conv_W1)
    wa = np.zeros((C, PARTS, HID), w1.dtype)
    for part in range(PARTS):
        kind = part % KINDS
        wa[:, part] = w1[:, kind * C:(kind + 1) * C].T
    wa = wa.reshape(KROWS, HID)
    w2t = np.asarray(L0_conv_W2).T
    w2 = np.zeros((HID, 2, 32), w2t.dtype)
    w2[:, 0, :C] = w2t
    w2[:, 1, C:] = w2t
    c1, c2 = np.asarray(L1_conv_w1), np.asarray(L1_conv_w2)
    g1 = np.stack([band(c1, p) for p in range(3)], axis=2)
    g2 = np.stack([band(c2, p) for p in range(3)], axis=2)
    g1v = np.stack([band(c1, 0, (1,)), band(c1, 0, (0,))], axis=1)

    bias = np.zeros((128, 6), x.dtype)
    bias[:, BI_HID] = np.asarray(L0_conv_b1)
    bias[:, BI_DELTA] = np.tile(np.asarray(L0_conv_b2), 8)
    for col in (BI_C1, BI_C1_TOP, BI_C1_LAST):
        bias[:, col] = np.tile(np.asarray(L1_conv_b1), 8)
    bias[96:112, BI_C1_TOP] = 0
    bias[112:128, BI_C1_LAST] = 0
    bias[:, BI_C2] = np.tile(np.asarray(L1_conv_b2), 8)

    nc = bacc.Bacc("TRN2", target_bir_lowering=False, num_devices=1)
    arrays = {"in_xs": xs, "in_xl": xl, "in_ru": ru, "in_wa": wa, "in_w2": w2, "in_g1": g1, "in_g1v": g1v,
              "in_g2": g2, "in_bias": bias}
    args = [nc.dram_tensor(name, a.shape, mybir.dt.from_np(a.dtype), kind="ExternalInput").ap()
            for name, a in arrays.items()]
    out = nc.dram_tensor("out", (NPAIR, 128, N), mybir.dt.float32, kind="ExternalOutput").ap()
    build_program(nc, *args, out)
    got = run_bass_kernel_spmd(nc, [arrays], core_ids=[0]).results[0]["out"]
    got = got.reshape(B, PAIRS, ROWS, C, 2, W).transpose(0, 3, 1, 4, 2, 5)
    return np.ascontiguousarray(got).reshape(B, C, H, W)
```

```python
from contextlib import ExitStack

import numpy as np

import concourse.bass as bass
from concourse import mybir

B, C, H, W = 32, 16, 256, 256
HID = 128
ROWS = 8
TILES = H // ROWS
PAIRS = TILES // 2
BLOCKS = PAIRS // 2
STRIP = 4
WP = W + 2
KINDS = 3
PARTS = 2 * KINDS
KROWS = PARTS * C
NPAIR = B * PAIRS
NBLOCK = B * BLOCKS
N = 2 * W
ALPHA = 3
XRING, ORING, YRING = 8, 2, 4
CHUNKS = 4

LAG_XP = 1
LAG_ROWS = 2
LAG_POOL = 3
LAG_ALIVE = 4
LAG_C1 = 5
LAG_C2 = 6

BI_HID, BI_DELTA, BI_C1, BI_C1_TOP, BI_C1_LAST, BI_C2 = range(6)


def build_program(nc, xs_d, xl_d, ru_d, wa_d, w2_d, g1_d, g1v_d, g2_d, bias_d, out_d):
    f32, f32r, bf16 = mybir.dt.float32, mybir.dt.float32r, mybir.dt.bfloat16
    ALU = mybir.AluOpType
    ACT = mybir.ActivationFunctionType

    alpha_d = nc.dram_tensor("alpha_scratch", (B, H + 2, W), f32).ap()
    mask_d = nc.dram_tensor("mask_scratch", (B, PAIRS, ROWS, 2, W), bf16).ap()

    ctx = ExitStack()
    with ctx:
        def sb(name, shape, dt=f32):
            return ctx.enter_context(nc.sbuf_tensor(name, shape, dt))

        def pb(name, shape):
            return ctx.enter_context(nc.psum_tensor(name, shape, f32))

        def sem(name):
            return ctx.enter_context(nc.semaphore(name))

        wa = sb("wa", [KROWS, HID])
        wa_hi = sb("wa_hi", [KROWS, HID], f32r)
        wa_lo = sb("wa_lo", [KROWS, HID], f32r)
        w2 = sb("w2", [HID, 2, 32])
        g1 = sb("g1", [128, 3, 3, 32])
        g1v = sb("g1v", [128, 2, 3, 32])
        g2 = sb("g2", [128, 3, 3, 32])
        bias = sb("bias", [128, 6])
        upd = sb("upd", [128, TILES, W], bf16)
        xs = sb("xs", [128, 2, STRIP + 2, WP])
        diff = sb("diff", [128, STRIP + 2, WP])
        duo = sb("duo", [128, STRIP + 1, W + 1])
        sx = sb("sx", [128, STRIP, W])
        sy = sb("sy", [128, STRIP, W])
        parts = sb("parts", [128, 2, PARTS, STRIP * W], f32r)
        perc = sb("perc", [KROWS, 2, 2, ROWS, W], f32r)
        hid = sb("hid", [HID, ROWS, N])
        delta = sb("delta", [128, N])
        x = sb("x", [128, XRING, 2, WP])
        nb = sb("nb", [16, 2, 3, WP])
        m1 = sb("m1", [16, WP])
        m2 = sb("m2", [16, WP])
        m3 = sb("m3", [16, W])
        m4 = sb("m4", [16, W])
        alive = sb("alive", [16, 2, W], bf16)
        alive_b = sb("alive_b", [128, 2, 2, W], bf16)
        st0 = sb("st0", [128, WP])
        st1 = sb("st1", [128, 4, WP])
        st2 = sb("st2", [128, 4, WP])
        o1 = sb("o1", [128, ORING, 2, WP])
        y = sb("y", [128, YRING, N])

        ps_hid = [pb(f"ps_hid{n}", [HID, 2, N]) for n in range(2)]
        ps_delta = pb("ps_delta", [128, N])
        ps_c1 = pb("ps_c1", [128, N])
        ps_c2 = pb("ps_c2", [128, N])
        ps_top = pb("ps_top", [128, N])

        s_const = sem("s_const")
        s_ru = sem("s_ru")
        s_upd = sem("s_upd")
        s_zero = sem("s_zero")
        s_wsplit = sem("s_wsplit")
        s_alpha0 = sem("s_alpha0")
        s_xs = [sem(f"s_xs{n}") for n in range(2)]
        s_xl = [sem(f"s_xl{n}") for n in range(2)]
        s_dx = sem("s_dx")
        s_tx = sem("s_tx")
        s_sx = sem("s_sx")
        s_dy = sem("s_dy")
        s_ty = sem("s_ty")
        s_sy = sem("s_sy")
        s_hi = [sem(f"s_hi{n}") for n in range(KINDS)]
        s_lo = [sem(f"s_lo{n}") for n in range(KINDS)]
        s_perc = [sem(f"s_perc{n}") for n in range(2)]
        s_hmm = sem("s_hmm")
        s_hev = sem("s_hev")
        s_dmm = sem("s_dmm")
        s_dev = sem("s_dev")
        s_x1 = sem("s_x1")
        s_aw = sem("s_aw")
        s_nb = [sem(f"s_nb{n}") for n in range(2)]
        s_m1, s_m2, s_m3, s_m4 = (sem(f"s_m{n}") for n in range(1, 5))
        s_alive = sem("s_alive")
        s_mw = sem("s_mw")
        s_mb = [sem(f"s_mb{n}") for n in range(2)]
        s_x2 = sem("s_x2")
        s_st0 = sem("s_st0")
        s_st1 = sem("s_st1")
        s_c1 = sem("s_c1")
        s_top = sem("s_top")
        s_topev = sem("s_topev")
        s_o1 = sem("s_o1")
        s_c2 = sem("s_c2")
        s_y = sem("s_y")
        s_out = [sem(f"s_out{n}") for n in range(2)]
        s_sp_gate = sem("s_sp_gate")

        block = ctx.enter_context(nc.Block())

        def val(i, per_image, offset):
            return i * per_image + offset

        def after(eng, semaphore, i, per_image, offset):
            v = val(i, per_image, offset)
            if isinstance(i, int) and v <= 0:
                return
            eng.wait_ge(semaphore, v)

        def gated(eng, gate, semaphore, i, per_image, offset):
            v = val(i, per_image, offset)
            if isinstance(i, int):
                if v > 0:
                    eng.wait_ge(semaphore, v)
                return
            eng.wait_ge(semaphore, v)
            eng.sem_inc(gate, 1)

        def there(i, q, of=NPAIR, per_image=PAIRS):
            return not isinstance(i, int) or 0 <= i * per_image + q < of

        def walk(eng, step):
            for s in range(-6, PAIRS):
                step(0, s)
            with eng.Fori(1, B - 1) as i:
                for j in range(PAIRS):
                    step(i, j)
            for j in range(PAIRS + LAG_C2 + 4):
                step(B - 1, j)

        @block.sync
        def _(sp):
            for dst, src in ((wa, wa_d), (w2, w2_d), (g1, g1_d), (g1v, g1v_d), (g2, g2_d), (bias, bias_d)):
                sp.dma_start(dst[:], src).then_inc(s_const, 16)
            half = TILES // 2 * W
            for n in range(2):
                if n:
                    sp.wait_ge(s_upd, n)
                sp.dma_start(
                    hid[:].rearrange("p r n -> p (r n)"),
                    ru_d[:, n * half:(n + 1) * half].unsqueeze(1).to_broadcast([ROWS, C, half]),
                ).then_inc(s_ru, 16)
            sp.wait_ge(s_zero, 1)
            sp.dma_start(alpha_d[:, 0:H + 2:H + 1, :], st1[0:B, 0:2, 0:W]).then_inc(s_alpha0, 16)

            def load_block(i, b):
                if not there(i, b, NBLOCK, BLOCKS):
                    return
                gated(sp, s_sp_gate, s_dy, i, BLOCKS, b - 1)
                gated(sp, s_sp_gate, s_lo[2], i, BLOCKS, b - 1)
                sp.dma_start(xs[:, b % 2].rearrange("p r w -> p (r w)"),
                             xs_d[val(i, BLOCKS, b)]).then_inc(s_xs[b % 2], 16)

            def load_pairs(i, q):
                if not there(i, q):
                    return
                gated(sp, s_sp_gate, s_y, i, PAIRS, q + 1 - XRING + 1)
                slot = q % XRING
                sp.dma_start(x[:, slot:slot + 2, :, 1:1 + W].rearrange("p q t w -> p (q t) w"),
                             xl_d[val(i, BLOCKS, q // 2)].rearrange("p (t w) -> p t w", t=4)
                             ).then_inc(s_xl[q // 2 % 2], 16)

            def write_alpha(i, q):
                if not there(i, q):
                    return
                gated(sp, s_sp_gate, s_x1, i, PAIRS, q + 1)
                img, j = i + q // PAIRS, q % PAIRS
                rows = alpha_d[img, 1 + 16 * j:1 + 16 * j + 16, :].rearrange("(t r) w -> r t w", t=2)
                sp.dma_start(rows, x[ALPHA::C, q % XRING, :, 1:1 + W]).then_inc(s_aw, 16)

            def load_neighbours(i, q):
                if not there(i, q):
                    return
                img, j = i + q // PAIRS, q % PAIRS
                below = 2 if j < PAIRS - 1 else 1
                gated(sp, s_sp_gate, s_aw, i, 16 * PAIRS, 16 * (q + below))
                gated(sp, s_sp_gate, s_m2, i, PAIRS, q - 1)
                src = alpha_d[img, 16 * j:16 * j + 16, :]
                src = bass.AP(tensor=src.tensor, offset=src.offset, ap=[[W, 16], [W, 3], [1, W]])
                sp.dma_start(nb[:, q % 2, :, 1:1 + W], src).then_inc(s_nb[q % 2], 16)

            def write_mask(i, q):
                if not there(i, q):
                    return
                gated(sp, s_sp_gate, s_alive, i, PAIRS, q + 1)
                img, j = i + q // PAIRS, q % PAIRS
                sp.dma_start(mask_d[img, j].rearrange("r t w -> t r w"), alive[:, q % 2, :]).then_inc(s_mw, 16)

            def load_mask(i, q):
                if not there(i, q):
                    return
                img, j = i + q // PAIRS, q % PAIRS
                gated(sp, s_sp_gate, s_mw, i, 16 * PAIRS, 16 * (q + 1))
                gated(sp, s_sp_gate, s_x2, i, PAIRS, q - 1)
                src = mask_d[img, j].rearrange("r t w -> r (t w)").unsqueeze(1).to_broadcast([ROWS, C, N])
                sp.dma_start(alive_b[:, q % 2].rearrange("p t w -> p (t w)"), src).then_inc(s_mb[q % 2], 16)

            def store_pairs(i, q):
                if not there(i, q):
                    return
                gated(sp, s_sp_gate, s_y, i, PAIRS, q + 2)
                slot = q % YRING
                sp.dma_start(out_d[val(i, BLOCKS, q // 2)],
                             y[:, slot:slot + 2, :].rearrange("p q n -> p (q n)")).then_inc(s_out[q // 2 % 2], 16)

            def step(i, j):
                even = j % 2 == 0
                write_alpha(i, j - LAG_XP)
                write_mask(i, j - LAG_POOL)
                if even:
                    load_pairs(i, j)
                load_neighbours(i, j - LAG_ROWS)
                load_mask(i, j - LAG_POOL)
                if even:
                    load_block(i, (j + 6) // 2)
                    store_pairs(i, j - LAG_C2 - 2)

            sp.wait_ge(s_zero, 2)
            sp.wait_ge(s_alpha0, 16)
            walk(sp, step)
            for n in range(2):
                sp.wait_ge(s_out[n], 16 * NBLOCK // 2)

        @block.gpsimd
        def _(pool):
            def sobel_x(i, b):
                if not there(i, b, NBLOCK, BLOCKS):
                    return
                src = xs[:, b % 2]
                after(pool, s_xs[b % 2], i, 16 * BLOCKS // 2, 16 * (b // 2 + 1))
                after(pool, s_ty, i, BLOCKS, b)
                pool.tensor_tensor(diff[:, :, 0:W], src[:, :, 2:WP], src[:, :, 0:W], ALU.subtract).then_inc(s_dx, 1)
                after(pool, s_dx, i, BLOCKS, b + 1)
                after(pool, s_sy, i, BLOCKS, b)
                pool.tensor_tensor(duo[:, :, 0:W], diff[:, 0:STRIP + 1, 0:W], diff[:, 1:STRIP + 2, 0:W],
                                   ALU.add).then_inc(s_tx, 1)
                after(pool, s_tx, i, BLOCKS, b + 1)
                after(pool, s_lo[0], i, BLOCKS, b)
                pool.tensor_tensor(sx[:], duo[:, 0:STRIP, 0:W], duo[:, 1:STRIP + 1, 0:W], ALU.add).then_inc(s_sx, 1)

            def sobel_y(i, b):
                if not there(i, b, NBLOCK, BLOCKS):
                    return
                src = xs[:, b % 2]
                after(pool, s_tx, i, BLOCKS, b + 1)
                pool.tensor_tensor(diff[:, 0:STRIP, :], src[:, 2:STRIP + 2, :], src[:, 0:STRIP, :],
                                   ALU.subtract).then_inc(s_dy, 1)
                after(pool, s_dy, i, BLOCKS, b + 1)
                after(pool, s_sx, i, BLOCKS, b + 1)
                pool.tensor_tensor(duo[:, 0:STRIP, 0:W + 1], diff[:, 0:STRIP, 0:W + 1], diff[:, 0:STRIP, 1:WP],
                                   ALU.add).then_inc(s_ty, 1)
                after(pool, s_ty, i, BLOCKS, b + 1)
                after(pool, s_lo[1], i, BLOCKS, b)
                pool.tensor_tensor(sy[:], duo[:, 0:STRIP, 0:W], duo[:, 0:STRIP, 1:1 + W], ALU.add).then_inc(s_sy, 1)

            def step(i, j):
                if j % 2 == 0:
                    sobel_x(i, (j + 4) // 2)
                else:
                    sobel_y(i, (j + 3) // 2)

            walk(pool, step)

        @block.scalar
        def _(act):
            def hidden(i, q, m):
                if not there(i, q):
                    return
                after(act, s_hmm, i, CHUNKS * PAIRS, CHUNKS * q + m + 1)
                if m == 0:
                    after(act, s_dmm, i, PAIRS, q)
                nc.scalar.activation(hid[:, 2 * m:2 * m + 2, :], ps_hid[m % 2][:], ACT.Relu,
                                     bias=bias[:, BI_HID:BI_HID + 1]).then_inc(s_hev, 1)

            def gather_perception(i, q):
                if not there(i, q):
                    return
                b = q // 2
                for kind in range(KINDS):
                    after(act, s_lo[kind], i, BLOCKS, b + 1)
                after(act, s_hmm, i, CHUNKS * PAIRS, CHUNKS * (q - 1))
                for n in range(4):
                    g = 4 * (q % 2) + n
                    act.dma_start(
                        perc[:, q % 2, n // 2, STRIP * (n % 2):STRIP * (n % 2 + 1), :].rearrange("k r w -> k (r w)").bitcast(f32),
                        parts[C * g:C * g + C, b % 2, :, :].bitcast(f32),
                    ).then_inc(s_perc[q % 2], 16)

            def conv1_out(i, q):
                if not there(i, q):
                    return
                j, slot = q % PAIRS, q % ORING
                tile = 2 * q % 4

                def relu(out, src, first, column=BI_C1):
                    return nc.scalar.activation(out, src, ACT.Relu,
                                                bias=bias[first:first + src.shape[0], column:column + 1])

                after(act, s_c2, i, PAIRS, q - 1)
                if j == 0:
                    after(act, s_top, i, 1, q // PAIRS + 1)
                    relu(st2[0:32, tile, 1:1 + W], ps_top[96:128, 0:W], 96, BI_C1_TOP).then_inc(s_topev, 1)
                after(act, s_c1, i, PAIRS, q + 1)
                src = ps_c1[:].rearrange("p (t w) -> p t w", t=2)
                relu(st2[32:64, tile:tile + 2, 1:1 + W], src[0:32], 0)
                if j == PAIRS - 1:
                    relu(st2[0:32, tile + 1, 1:1 + W], src[96:128, 0], 96)
                    relu(o1[:, slot, 0, 1:1 + W], src[:, 0], 0)
                    relu(o1[:, slot, 1, 1:1 + W], src[:, 1], 0, BI_C1_LAST).then_inc(s_o1, 1)
                    return
                if tile == 0:
                    relu(st2[0:32, 1:3, 1:1 + W], src[96:128], 96)
                else:
                    relu(st2[0:32, 3, 1:1 + W], src[96:128, 0], 96)
                    relu(st2[0:32, 0, 1:1 + W], src[96:128, 1], 96)
                relu(o1[:, slot, :, 1:1 + W], src, 0).then_inc(s_o1, 1)

            def step(i, j):
                hidden(i, j, 0)
                hidden(i, j, 1)
                gather_perception(i, j + 1)
                hidden(i, j, 2)
                hidden(i, j, 3)
                conv1_out(i, j - LAG_C1)

            act.wait_ge(s_const, 96)
            act.wait_ge(s_upd, 2)
            act.wait_ge(s_zero, 2)
            walk(act, step)

        @block.vector
        def _(dve):
            dve.memset(st1[:], 0.0).then_inc(s_zero, 1)
            for buf in (x, o1, st2, st0):
                dve.memset(buf[:], 0.0)
            dve.memset(nb[:], 0.0).then_inc(s_zero, 1)
            half = TILES // 2
            for n in range(2):
                dve.wait_ge(s_ru, 16 * (n + 1))
                dve.tensor_scalar(upd[:, n * half:(n + 1) * half, :].rearrange("p t w -> p (t w)"),
                                  hid[:].rearrange("p r n -> p (r n)"), 0.5, None, ALU.is_lt).then_inc(s_upd, 1)
            dve.wait_ge(s_const, 96)
            dve.tensor_copy(wa_hi[:], wa[:]).then_inc(s_wsplit, 1)
            dve.wait_ge(s_wsplit, 1)
            dve.tensor_tensor(wa_lo[:], wa[:], wa_hi[:].bitcast(f32), ALU.subtract).then_inc(s_wsplit, 1)
            dve.wait_ge(s_upd, 2)

            def source(kind, b):
                return (sx[:], sy[:], xs[:, b % 2, 1:1 + STRIP, 1:1 + W])[kind]

            def part(kind, b, dt=f32r):
                return parts[:, b % 2, kind, :].rearrange("p (r w) -> p r w", r=STRIP)

            def split_hi(i, b, kind):
                if not there(i, b, NBLOCK, BLOCKS):
                    return
                if kind == 0:
                    after(dve, s_sx, i, BLOCKS, b + 1)
                elif kind == 1:
                    after(dve, s_sy, i, BLOCKS, b + 1)
                else:
                    after(dve, s_xs[b % 2], i, 16 * BLOCKS // 2, 16 * (b // 2 + 1))
                    for n in range(2):
                        after(dve, s_perc[n], i, 64 * BLOCKS, 64 * (b - 1))
                dve.tensor_copy(part(kind, b), source(kind, b)).then_inc(s_hi[kind], 1)

            def split_lo(i, b, kind):
                if not there(i, b, NBLOCK, BLOCKS):
                    return
                after(dve, s_hi[kind], i, BLOCKS, b + 1)
                dve.tensor_tensor(part(KINDS + kind, b), source(kind, b), part(kind, b).bitcast(f32),
                                  ALU.subtract).then_inc(s_lo[kind], 1)

            def masked_delta(i, q):
                if not there(i, q):
                    return
                j = q % PAIRS
                after(dve, s_dmm, i, PAIRS, q + 1)
                after(dve, s_x1, i, PAIRS, q)
                dve.scalar_tensor_tensor(out=delta[:], in0=ps_delta[:], scalar=bias[:, BI_DELTA:BI_DELTA + 1],
                                         in1=upd[:, 2 * j:2 * j + 2, :].rearrange("p t w -> p (t w)"),
                                         op0=ALU.add, op1=ALU.mult).then_inc(s_dev, 1)

            def make_x1(i, q):
                if not there(i, q):
                    return
                after(dve, s_dev, i, PAIRS, q + 1)
                after(dve, s_xl[q // 2 % 2], i, 16 * BLOCKS // 2, 16 * (q // 4 + 1))
                here = x[:, q % XRING, :, 1:1 + W]
                dve.tensor_tensor(here, here, delta[:].rearrange("p (t w) -> p t w", t=2), ALU.add).then_inc(s_x1, 1)

            def make_alive(i, q):
                if not there(i, q):
                    return
                rows = nb[:, q % 2]
                after(dve, s_nb[q % 2], i, 16 * PAIRS // 2, 16 * (q // 2 + 1))
                dve.tensor_tensor(m1[:], rows[:, 0], rows[:, 1], ALU.max).then_inc(s_m1, 1)
                after(dve, s_m1, i, PAIRS, q + 1)
                dve.tensor_tensor(m2[:], m1[:], rows[:, 2], ALU.max).then_inc(s_m2, 1)
                after(dve, s_m2, i, PAIRS, q + 1)
                dve.tensor_tensor(m3[:], m2[:, 0:W], m2[:, 1:1 + W], ALU.max).then_inc(s_m3, 1)
                after(dve, s_m3, i, PAIRS, q + 1)
                dve.tensor_tensor(m4[:], m3[:], m2[:, 2:WP], ALU.max).then_inc(s_m4, 1)
                after(dve, s_m4, i, PAIRS, q + 1)
                after(dve, s_mw, i, 16 * PAIRS, 16 * (q - 1))
                dve.tensor_scalar(alive[:, q % 2, :], m4[:], 0.1, None, ALU.is_gt).then_inc(s_alive, 1)

            def apply_alive(i, q):
                if not there(i, q):
                    return
                j, slot, tile = q % PAIRS, q % XRING, 2 * q % 4
                after(dve, s_mb[q % 2], i, 16 * PAIRS // 2, 16 * (q // 2 + 1))
                after(dve, s_aw, i, 16 * PAIRS, 16 * (q + 1))
                here = x[:, slot, :, 1:1 + W]
                dve.tensor_tensor(here, here, alive_b[:, q % 2], ALU.mult).then_inc(s_x2, 1)
                after(dve, s_x2, i, PAIRS, q + 1)
                after(dve, s_c1, i, PAIRS, q - 1)
                dve.tensor_copy(st1[0:32, tile:tile + 2, :], x[96:128, slot])
                if j == 0:
                    dve.tensor_copy(st0[32:64, :], x[0:32, slot, 0]).then_inc(s_st0, 1)
                    dve.tensor_copy(st1[32:64, tile, :], x[0:32, slot, 1])
                elif tile:
                    dve.tensor_copy(st1[32:64, 1:3, :], x[0:32, slot]).then_inc(s_st1, 1)
                else:
                    dve.tensor_copy(st1[32:64, 0, :], x[0:32, slot, 1])
                    dve.tensor_copy(st1[32:64, 3, :], x[0:32, slot, 0]).then_inc(s_st1, 1)
                if j == PAIRS - 1:
                    dve.memset(st1[32:64, tile + 1, :], 0.0).then_inc(s_st1, 1)

            def output(i, q):
                if not there(i, q):
                    return
                after(dve, s_c2, i, PAIRS, q + 1)
                after(dve, s_x2, i, PAIRS, q + 1)
                after(dve, s_out[q // 2 % 2], i, 16 * BLOCKS // 2, 16 * (q // 4))
                dve.scalar_tensor_tensor(out=y[:, q % YRING].rearrange("p (t w) -> p t w", t=2),
                                         in0=ps_c2[:].rearrange("p (t w) -> p t w", t=2),
                                         scalar=bias[:, BI_C2:BI_C2 + 1], in1=x[:, q % XRING, :, 1:1 + W],
                                         op0=ALU.add, op1=ALU.add).then_inc(s_y, 1)

            def step(i, j):
                odd = j % 2
                b = (j + 3) // 2 if odd else (j + 2) // 2
                masked_delta(i, j - LAG_XP)
                split_hi(i, b, 2 if odd else 1)
                make_x1(i, j - LAG_XP)
                apply_alive(i, j - LAG_ALIVE)
                make_alive(i, j - LAG_POOL)
                if odd:
                    split_hi(i, b, 0)
                split_lo(i, b, 2 if odd else 1)
                output(i, j - LAG_C2)
                if odd:
                    split_lo(i, b, 0)

            walk(dve, step)

        @block.tensor
        def _(pe):
            def hidden(i, q, m):
                if not there(i, q):
                    return
                if m == 0:
                    after(pe, s_perc[q % 2], i, 64 * PAIRS // 2, 64 * (q // 2 + 1))
                after(pe, s_hev, i, CHUNKS * PAIRS, CHUNKS * q + m - 1)
                for n in range(2):
                    r = 2 * m + n
                    rhs = perc[:, q % 2, :, r, :]
                    out = ps_hid[m % 2][:, n, :]
                    nc.tensor.matmul(out, wa_hi[:], rhs, start=True, stop=False)
                    last = nc.tensor.matmul(out, wa_lo[:], rhs, start=False, stop=True)
                last.then_inc(s_hmm, 1)

            def delta_products(i, q):
                if not there(i, q):
                    return
                after(pe, s_hev, i, CHUNKS * PAIRS, CHUNKS * (q + 1))
                after(pe, s_dev, i, PAIRS, q)
                for n in range(2):
                    for t in range(4):
                        last = nc.tensor.matmul(ps_delta[32 * t:32 * t + 32, :], w2[:, n, :], hid[:, 2 * t + n, :],
                                                start=(n == 0), stop=(n == 1))
                last.then_inc(s_dmm, 1)

            def conv1(i, q):
                if not there(i, q):
                    return
                j, slot = q % PAIRS, q % XRING
                after(pe, s_x2, i, PAIRS, q + 1)
                after(pe, s_o1, i, PAIRS, q)
                if j == 0:
                    after(pe, s_st0, i, 1, q // PAIRS + 1)
                    after(pe, s_topev, i, 1, q // PAIRS)
                    for dx in range(3):
                        last = nc.tensor.matmul(ps_top[96:128, 0:W], g1v[:, 0, dx, :], st0[:, dx:dx + W],
                                                start=(dx == 0), stop=(dx == 2), tile_position=(0, 96))
                    last.then_inc(s_top, 1)
                after(pe, s_st1, i, PAIRS, q + 1)
                tile = 2 * q % 4
                halves = j == PAIRS - 1
                for dx in range(3):
                    for t in range(3):
                        last = nc.tensor.matmul(ps_c1[32 * t:32 * t + 32, :], g1[:, dx, t, :],
                                                x[:, slot, :, dx:dx + W], start=(dx == 0), stop=(dx == 2))
                    if not halves:
                        last = nc.tensor.matmul(ps_c1[96:128, :], g1[:, dx, 0, :], st1[:, tile:tile + 2, dx:dx + W],
                                                start=(dx == 0), stop=(dx == 2), tile_position=(0, 96))
                if halves:
                    for t in range(2):
                        for dx in range(3):
                            lhs = g1v[:, 1, dx, :] if t else g1[:, dx, 0, :]
                            last = nc.tensor.matmul(ps_c1[96:128, t * W:(t + 1) * W], lhs, st1[:, tile + t, dx:dx + W],
                                                    start=(dx == 0), stop=(dx == 2), tile_position=(0, 96))
                last.then_inc(s_c1, 1)

            def conv2(i, q):
                if not there(i, q):
                    return
                slot = q % ORING
                tile = 2 * q % 4
                after(pe, s_o1, i, PAIRS, q + 1)
                after(pe, s_y, i, PAIRS, q)
                for dx in range(3):
                    for t in range(4):
                        rhs = o1[:, slot, :, dx:dx + W] if t else st2[:, tile:tile + 2, dx:dx + W]
                        last = nc.tensor.matmul(ps_c2[32 * t:32 * t + 32, :], g2[:, dx, max(t - 1, 0), :], rhs,
                                                start=(dx == 0), stop=(dx == 2), tile_position=(0, 32 * t))
                last.then_inc(s_c2, 1)

            def step(i, j):
                hidden(i, j, 0)
                hidden(i, j, 1)
                conv2(i, j - LAG_C2)
                hidden(i, j, 2)
                hidden(i, j, 3)
                conv1(i, j - LAG_C1)
                delta_products(i, j)

            pe.wait_ge(s_const, 96)
            pe.wait_ge(s_wsplit, 2)
            pe.wait_ge(s_zero, 2)
            walk(pe, step)


def band(w, place, first_rows=(0, 1)):
    out = np.zeros((128, 3, 32), w.dtype)
    for a in range(4):
        for r in first_rows:
            if 0 <= a - r <= 2:
                k = 32 * place + C * a
                out[k:k + C, :, C * r:C * r + C] = w[:, :, a - r, :].transpose(1, 2, 0)
    return out


def kernel(x, L0_conv_rand_u, L0_conv_W1, L0_conv_b1, L0_conv_W2, L0_conv_b2,
           L1_conv_w1, L1_conv_b1, L1_conv_w2, L1_conv_b2):
    import concourse.bacc as bacc
    from concourse.bass_utils import run_bass_kernel_spmd

    x = np.asarray(x)
    padded = np.zeros((B, C, H + 2, WP), x.dtype)
    padded[:, :, 1:-1, 1:-1] = x
    strips = np.lib.stride_tricks.sliding_window_view(padded, STRIP + 2, axis=2)[:, :, ::STRIP]
    strips = strips.reshape(B, C, BLOCKS, 8, WP, STRIP + 2).transpose(0, 2, 3, 1, 5, 4)
    xs = np.ascontiguousarray(strips).reshape(NBLOCK, 128, (STRIP + 2) * WP)
    xl = np.ascontiguousarray(x.reshape(B, C, PAIRS, 2, ROWS, W).transpose(0, 2, 4, 1, 3, 5)).reshape(NPAIR, 128, N)
    xl = np.ascontiguousarray(xl.reshape(NBLOCK, 2, 128, N).transpose(0, 2, 1, 3)).reshape(NBLOCK, 128, 2 * N)
    ru = np.asarray(L0_conv_rand_u)
    ru = np.ascontiguousarray(ru.reshape(TILES, ROWS, W).transpose(1, 0, 2)).reshape(ROWS, TILES * W)

    w1 = np.asarray(L0_conv_W1)
    wa = np.zeros((C, PARTS, HID), w1.dtype)
    for part in range(PARTS):
        kind = part % KINDS
        wa[:, part] = w1[:, kind * C:(kind + 1) * C].T
    wa = wa.reshape(KROWS, HID)
    w2t = np.asarray(L0_conv_W2).T
    w2 = np.zeros((HID, 2, 32), w2t.dtype)
    w2[:, 0, :C] = w2t
    w2[:, 1, C:] = w2t
    c1, c2 = np.asarray(L1_conv_w1), np.asarray(L1_conv_w2)
    g1 = np.stack([band(c1, p) for p in range(3)], axis=2)
    g2 = np.stack([band(c2, p) for p in range(3)], axis=2)
    g1v = np.stack([band(c1, 0, (1,)), band(c1, 0, (0,))], axis=1)

    bias = np.zeros((128, 6), x.dtype)
    bias[:, BI_HID] = np.asarray(L0_conv_b1)
    bias[:, BI_DELTA] = np.tile(np.asarray(L0_conv_b2), 8)
    for col in (BI_C1, BI_C1_TOP, BI_C1_LAST):
        bias[:, col] = np.tile(np.asarray(L1_conv_b1), 8)
    bias[96:112, BI_C1_TOP] = 0
    bias[112:128, BI_C1_LAST] = 0
    bias[:, BI_C2] = np.tile(np.asarray(L1_conv_b2), 8)

    nc = bacc.Bacc("TRN2", target_bir_lowering=False, num_devices=1)
    arrays = {"in_xs": xs, "in_xl": xl, "in_ru": ru, "in_wa": wa, "in_w2": w2, "in_g1": g1, "in_g1v": g1v,
              "in_g2": g2, "in_bias": bias}
    args = [nc.dram_tensor(name, a.shape, mybir.dt.from_np(a.dtype), kind="ExternalInput").ap()
            for name, a in arrays.items()]
    out = nc.dram_tensor("out", (NBLOCK, 128, 2 * N), mybir.dt.float32, kind="ExternalOutput").ap()
    build_program(nc, *args, out)
    got = run_bass_kernel_spmd(nc, [arrays], core_ids=[0]).results[0]["out"]
    got = got.reshape(B, BLOCKS, ROWS, C, 2, 2, W).transpose(0, 3, 1, 4, 5, 2, 6)
    return np.ascontiguousarray(got).reshape(B, C, H, W)
```

```python
from contextlib import ExitStack

import numpy as np

import concourse.bass as bass
from concourse import mybir

B, C, H, W = 32, 16, 256, 256
HID = 128
TROWS = 4
TP = 4
PAIRS = H // (TROWS * TP)
GROUPS = 8
HALF = 64
BLOCKS = PAIRS // 2
STRIP = 4
WP = W + 2
WH = W // 2
HP = WH + 2
KINDS = 3
PARTS = 2 * KINDS
KROWS = PARTS * C
NPAIR = B * PAIRS
NBLOCK = B * BLOCKS
N = TP * WH
ALPHA = 3
XRING, ORING, YRING = 8, 2, 4
CHUNKS = TP

LAG_XP = 1
LAG_ROWS = 2
LAG_POOL = 3
LAG_ALIVE = 4
LAG_C1 = 5
LAG_C2 = 6

BI_HID, BI_DELTA, BI_C1, BI_C1_TOP, BI_C1_LAST, BI_C2 = range(6)


def build_program(nc, xs_d, xl_d, ru_d, wa_d, w2_d, g1_d, g1v_d, g2_d, bias_d, out_d):
    f32, f32r, bf16 = mybir.dt.float32, mybir.dt.float32r, mybir.dt.bfloat16
    ALU = mybir.AluOpType
    ACT = mybir.ActivationFunctionType

    alpha_d = nc.dram_tensor("alpha_scratch", (B, H // 2 + 2, 4, WH), bf16).ap()
    mask_d = nc.dram_tensor("mask_scratch", (B, PAIRS, GROUPS, TP, WH), bf16).ap()

    ctx = ExitStack()
    with ctx:
        def sb(name, shape, dt=f32):
            return ctx.enter_context(nc.sbuf_tensor(name, shape, dt))

        def pb(name, shape):
            return ctx.enter_context(nc.psum_tensor(name, shape, f32))

        def sem(name):
            return ctx.enter_context(nc.semaphore(name))

        wa = sb("wa", [KROWS, HID])
        wa_hi = sb("wa_hi", [KROWS, HID], f32r)
        wa_lo = sb("wa_lo", [KROWS, HID], f32r)
        w2 = sb("w2", [HID, 2, 32])
        g1 = sb("g1", [128, 2, 2, 2, 32])
        g1v = sb("g1v", [128, 2, 2, 2, 32])
        g2 = sb("g2", [128, 2, 2, 2, 32])
        bias = sb("bias", [128, 6])
        upd = sb("upd", [128, PAIRS, N], bf16)
        xs = sb("xs", [128, 2, STRIP + 2, WP])
        diff = sb("diff", [128, STRIP + 2, WP])
        duo = sb("duo", [128, STRIP + 1, W + 1])
        sx = sb("sx", [128, STRIP, 2, WH])
        sy = sb("sy", [128, STRIP, 2, WH])
        parts = sb("parts", [128, 2, PARTS, STRIP * W], f32r)
        perc = sb("perc", [KROWS, 2, TP, TROWS, 2, WH], f32r)
        hid = sb("hid", [HID, GROUPS, N])
        delta = sb("delta", [128, N])
        x = sb("x", [128, XRING, TP, HP])
        above = sb("above", [128, 2, N], bf16)
        nb = sb("nb", [8, 2, 3, 2, 2, HP], bf16)
        m1 = sb("m1", [8, 2, HP], bf16)
        m2 = sb("m2", [8, 2, 2, HP], bf16)
        m3 = sb("m3", [8, 2, WH], bf16)
        alive = sb("alive", [8, 2, 4 * WH], bf16)
        alive_b = sb("alive_b", [128, 2, N], bf16)
        st0 = sb("st0", [128, HP])
        st1 = sb("st1", [128, 2 * TP, HP])
        st2 = sb("st2", [128, 2 * TP, HP])
        o1 = sb("o1", [128, ORING, TP, HP])
        y = sb("y", [128, YRING, N])

        ps_hid = [pb(f"ps_hid{n}", [HID, 2, N]) for n in range(2)]
        ps_delta = pb("ps_delta", [128, N])
        ps_c1 = pb("ps_c1", [128, N])
        ps_c2 = pb("ps_c2", [128, N])
        ps_top = pb("ps_top", [128, N])

        s_const = sem("s_const")
        s_ru = [sem(f"s_ru{n}") for n in range(2)]
        s_upd = sem("s_upd")
        s_zero = sem("s_zero")
        s_wsplit = sem("s_wsplit")
        s_alpha0 = sem("s_alpha0")
        s_xs = [sem(f"s_xs{n}") for n in range(2)]
        s_xl = [sem(f"s_xl{n}") for n in range(2)]
        s_dx = sem("s_dx")
        s_tx = sem("s_tx")
        s_sx = sem("s_sx")
        s_dy = sem("s_dy")
        s_ty = sem("s_ty")
        s_sy = sem("s_sy")
        s_hi = [sem(f"s_hi{n}") for n in range(KINDS)]
        s_lo = [sem(f"s_lo{n}") for n in range(KINDS)]
        s_perc = [[sem(f"s_perc{n}_{t}") for t in range(TP)] for n in range(2)]
        s_hmm = sem("s_hmm")
        s_hev = sem("s_hev")
        s_dmm = sem("s_dmm")
        s_dev = sem("s_dev")
        s_x1 = sem("s_x1")
        s_above = sem("s_above")
        s_aw = [sem(f"s_aw{n}") for n in range(2)]
        s_nb = [sem(f"s_nb{n}") for n in range(2)]
        s_m1, s_m2, s_m3 = (sem(f"s_m{n}") for n in range(1, 4))
        s_alive = sem("s_alive")
        s_mw = sem("s_mw")
        s_mb = [sem(f"s_mb{n}") for n in range(2)]
        s_x2 = sem("s_x2")
        s_st0 = sem("s_st0")
        s_st1 = sem("s_st1")
        s_c1 = sem("s_c1")
        s_top = sem("s_top")
        s_topev = sem("s_topev")
        s_o1 = sem("s_o1")
        s_c2 = sem("s_c2")
        s_y = sem("s_y")
        s_out = [sem(f"s_out{n}") for n in range(2)]
        s_sp_gate = sem("s_sp_gate")

        ru0 = hid[:].rearrange("p r n -> p (r n)")
        ru1 = x[:].rearrange("p q t w -> p (q t w)")

        block = ctx.enter_context(nc.Block())

        def val(i, per_image, offset):
            return i * per_image + offset

        def after(eng, semaphore, i, per_image, offset):
            v = val(i, per_image, offset)
            if isinstance(i, int) and v <= 0:
                return
            eng.wait_ge(semaphore, v)

        def gated(eng, gate, semaphore, i, per_image, offset):
            v = val(i, per_image, offset)
            if isinstance(i, int):
                if v > 0:
                    eng.wait_ge(semaphore, v)
                return
            eng.wait_ge(semaphore, v)
            eng.sem_inc(gate, 1)

        def there(i, q, of=NPAIR, per_image=PAIRS):
            return not isinstance(i, int) or 0 <= i * per_image + q < of

        def source(kind, b):
            columns = xs[:, b % 2, 1:1 + STRIP, 1:1 + W].rearrange("p r (h e) -> p r e h", e=2)
            return (sx[:], sy[:], columns)[kind]

        def part(kind, b):
            return parts[:, b % 2, kind, :].rearrange("p (r e h) -> p r e h", r=STRIP, e=2)

        def walk(eng, step):
            for s in range(-6, PAIRS):
                step(0, s)
            with eng.Fori(1, B - 1) as i:
                for j in range(PAIRS):
                    step(i, j)
            for j in range(PAIRS + LAG_C2 + 4):
                step(B - 1, j)

        @block.sync
        def _(sp):
            def load_block(i, b):
                if not there(i, b, NBLOCK, BLOCKS):
                    return
                gated(sp, s_sp_gate, s_dy, i, BLOCKS, b - 1)
                gated(sp, s_sp_gate, s_lo[2], i, BLOCKS, b - 1)
                sp.dma_start(xs[:, b % 2].rearrange("p r w -> p (r w)"),
                             xs_d[val(i, BLOCKS, b)]).then_inc(s_xs[b % 2], 16)

            load_block(0, 0)
            for dst, src in ((wa, wa_d), (w2, w2_d), (g1, g1_d), (g1v, g1v_d), (g2, g2_d), (bias, bias_d)):
                sp.dma_start(dst[:], src).then_inc(s_const, 16)
            half = PAIRS // 2 * N
            for n, buf in enumerate((ru0, ru1)):
                sp.dma_start(
                    buf[:, 0:half],
                    ru_d[:, n * half:(n + 1) * half].unsqueeze(1).to_broadcast([GROUPS, C, half]),
                ).then_inc(s_ru[n], 16)
                if n == 0:
                    load_block(0, 1)
            sp.wait_ge(s_zero, 1)
            sp.dma_start(alpha_d[:, 0:H // 2 + 2:H // 2 + 1].rearrange("b r g w -> b r (g w)"),
                         above[0:B]).then_inc(s_alpha0, 16)

            def load_pairs(i, q):
                if not there(i, q):
                    return
                gated(sp, s_sp_gate, s_y, i, PAIRS, q + 1 - XRING + 1)
                slot = q % XRING
                sp.dma_start(x[:, slot:slot + 2, :, 1:1 + WH].rearrange("p q t w -> p (q t) w"),
                             xl_d[val(i, BLOCKS, q // 2)].rearrange("p (t w) -> p t w", t=2 * TP)
                             ).then_inc(s_xl[q // 2 % 2], 16)

            def write_alpha(i, q):
                if not there(i, q):
                    return
                gated(sp, s_sp_gate, s_above, i, PAIRS, q + 1)
                img, j = i + q // PAIRS, q % PAIRS
                rows = alpha_d[img, 1 + 8 * j:1 + 8 * j + 8]
                rows = bass.AP(tensor=rows.tensor, offset=rows.offset, ap=[[WH, GROUPS], [GROUPS * WH, TP], [1, WH]])
                sp.dma_start(rows, above[ALPHA::C, q % 2].rearrange("p (t w) -> p t w", t=TP)
                             ).then_inc(s_aw[q % 2], 16)

            def load_neighbours(i, q):
                if not there(i, q):
                    return
                img, j = i + q // PAIRS, q % PAIRS
                for p in (q, q + 1) if j < PAIRS - 1 else (q,):
                    gated(sp, s_sp_gate, s_aw[p % 2], i, 16 * PAIRS // 2, 16 * (p // 2 + 1))
                gated(sp, s_sp_gate, s_m2, i, PAIRS, q - 1)
                src = alpha_d[img, 8 * j:8 * j + 8]
                src = bass.AP(tensor=src.tensor, offset=src.offset, ap=[[4 * WH, 8], [WH, 12], [1, WH]])
                sp.dma_start(nb[:, q % 2, :, :, :, 1:1 + WH].rearrange("p r e l w -> p (r e l) w"), src).then_inc(s_nb[q % 2], 16)

            def write_mask(i, q):
                if not there(i, q):
                    return
                gated(sp, s_sp_gate, s_alive, i, PAIRS, q + 1)
                img, j = i + q // PAIRS, q % PAIRS
                sp.dma_start(mask_d[img, j].rearrange("g t w -> t g w"), alive[:, q % 2, :]).then_inc(s_mw, 16)

            def load_mask(i, q):
                if not there(i, q):
                    return
                img, j = i + q // PAIRS, q % PAIRS
                gated(sp, s_sp_gate, s_mw, i, 16 * PAIRS, 16 * (q + 1))
                gated(sp, s_sp_gate, s_x2, i, PAIRS, q - 1)
                src = mask_d[img, j].rearrange("g t w -> g (t w)").unsqueeze(1).to_broadcast([GROUPS, C, N])
                sp.dma_start(alive_b[:, q % 2], src).then_inc(s_mb[q % 2], 16)

            def store_pairs(i, q):
                if not there(i, q):
                    return
                gated(sp, s_sp_gate, s_y, i, PAIRS, q + 2)
                slot = q % YRING
                sp.dma_start(out_d[val(i, BLOCKS, q // 2)],
                             y[:, slot:slot + 2, :].rearrange("p q n -> p (q n)")).then_inc(s_out[q // 2 % 2], 16)

            def step(i, j):
                even = j % 2 == 0
                write_alpha(i, j - LAG_XP)
                write_mask(i, j - LAG_POOL)
                if even:
                    load_pairs(i, j)
                elif not isinstance(i, int) or i or j > -3:
                    load_block(i, (j + 5) // 2)
                load_neighbours(i, j - LAG_ROWS)
                load_mask(i, j - LAG_POOL)
                if even:
                    store_pairs(i, j - LAG_C2 - 2)

            sp.wait_ge(s_zero, 2)
            sp.wait_ge(s_alpha0, 16)
            walk(sp, step)
            for n in range(2):
                sp.wait_ge(s_out[n], 16 * NBLOCK // 2)

        @block.gpsimd
        def _(pool):
            def columns(src):
                return src.rearrange("p r (h e) -> p r h e", e=2)

            def by_parity(dst):
                return dst[:].rearrange("p r e h -> p r h e")

            def sobel_x(i, b):
                if not there(i, b, NBLOCK, BLOCKS):
                    return
                src = xs[:, b % 2]
                after(pool, s_xs[b % 2], i, 16 * BLOCKS // 2, 16 * (b // 2 + 1))
                after(pool, s_ty, i, BLOCKS, b)
                pool.tensor_tensor(diff[:, :, 0:W], src[:, :, 2:WP], src[:, :, 0:W], ALU.subtract).then_inc(s_dx, 1)
                after(pool, s_dx, i, BLOCKS, b + 1)
                after(pool, s_sy, i, BLOCKS, b)
                pool.tensor_tensor(duo[:, :, 0:W], diff[:, 0:STRIP + 1, 0:W], diff[:, 1:STRIP + 2, 0:W],
                                   ALU.add).then_inc(s_tx, 1)
                after(pool, s_tx, i, BLOCKS, b + 1)
                after(pool, s_lo[0], i, BLOCKS, b)
                pool.tensor_tensor(by_parity(sx), columns(duo[:, 0:STRIP, 0:W]), columns(duo[:, 1:STRIP + 1, 0:W]),
                                   ALU.add).then_inc(s_sx, 1)

            def sobel_y(i, b):
                if not there(i, b, NBLOCK, BLOCKS):
                    return
                src = xs[:, b % 2]
                after(pool, s_tx, i, BLOCKS, b + 1)
                pool.tensor_tensor(diff[:, 0:STRIP, :], src[:, 2:STRIP + 2, :], src[:, 0:STRIP, :],
                                   ALU.subtract).then_inc(s_dy, 1)
                after(pool, s_dy, i, BLOCKS, b + 1)
                after(pool, s_sx, i, BLOCKS, b + 1)
                pool.tensor_tensor(duo[:, 0:STRIP, 0:W + 1], diff[:, 0:STRIP, 0:W + 1], diff[:, 0:STRIP, 1:WP],
                                   ALU.add).then_inc(s_ty, 1)
                after(pool, s_ty, i, BLOCKS, b + 1)
                after(pool, s_lo[1], i, BLOCKS, b)
                pool.tensor_tensor(by_parity(sy), columns(duo[:, 0:STRIP, 0:W]), columns(duo[:, 0:STRIP, 1:1 + W]),
                                   ALU.add).then_inc(s_sy, 1)

            def step(i, j):
                if j % 2 == 0:
                    sobel_x(i, (j + 4) // 2)
                else:
                    sobel_y(i, (j + 3) // 2)

            walk(pool, step)

        @block.scalar
        def _(act):
            def hidden(i, q, m):
                if not there(i, q):
                    return
                after(act, s_hmm, i, CHUNKS * PAIRS, CHUNKS * q + m + 1)
                if m == 0:
                    after(act, s_dmm, i, PAIRS, q)
                nc.scalar.activation(hid[:, :, m * WH:(m + 1) * WH],
                                     ps_hid[m % 2][:].rearrange("p n (g w) -> p (n g) w", w=WH), ACT.Relu,
                                     bias=bias[:, BI_HID:BI_HID + 1]).then_inc(s_hev, 1)

            def gather_perception(i, q, tiles):
                if not there(i, q):
                    return
                b = q // 2
                if 0 in tiles:
                    for kind in range(KINDS):
                        after(act, s_lo[kind], i, BLOCKS, b + 1)
                for t in tiles:
                    after(act, s_hmm, i, CHUNKS * PAIRS, CHUNKS * (q - 2) + t + 1)
                    g = TP * (q % 2) + t
                    act.dma_start(
                        perc[:, q % 2, t].rearrange("k r e w -> k (r e w)").bitcast(f32),
                        parts[C * g:C * g + C, b % 2, :, :].bitcast(f32),
                    ).then_inc(s_perc[q % 2][t], 16)

            def split_hi(i, b, kind):
                if not there(i, b, NBLOCK, BLOCKS):
                    return
                if kind == 0:
                    after(act, s_sx, i, BLOCKS, b + 1)
                elif kind == 1:
                    after(act, s_sy, i, BLOCKS, b + 1)
                else:
                    after(act, s_xs[b % 2], i, 16 * BLOCKS // 2, 16 * (b // 2 + 1))
                    for n in range(2):
                        for t in range(TP):
                            after(act, s_perc[n][t], i, 16 * BLOCKS, 16 * (b - 1))
                nc.scalar.activation(part(kind, b), source(kind, b), ACT.Copy).then_inc(s_hi[kind], 1)

            def conv1_out(i, q):
                if not there(i, q):
                    return
                j, slot = q % PAIRS, q % ORING
                tile = TP * (q % 2)

                def relu(out, src, first=0, column=BI_C1):
                    return nc.scalar.activation(out, src, ACT.Relu,
                                                bias=bias[first:first + src.shape[0], column:column + 1])

                after(act, s_c2, i, PAIRS, q - 1)
                if j == 0:
                    after(act, s_top, i, 1, q // PAIRS + 1)
                    relu(st2[HALF:128, tile, 1:1 + WH], ps_top[HALF:128, 0:WH], HALF, BI_C1_TOP).then_inc(s_topev, 1)
                after(act, s_c1, i, PAIRS, q + 1)
                src = ps_c1[:].rearrange("p (t w) -> p t w", t=TP)
                relu(st2[0:HALF, tile:tile + TP, 1:1 + WH], src[0:HALF])
                if tile == 0:
                    relu(st2[HALF:128, 1:1 + TP, 1:1 + WH], src[HALF:128], HALF)
                else:
                    relu(st2[HALF:128, tile + 1:tile + TP, 1:1 + WH], src[HALF:128, 0:TP - 1], HALF)
                if j == PAIRS - 1:
                    relu(o1[:, slot, 0:TP - 1, 1:1 + WH], src[:, 0:TP - 1])
                    relu(o1[:, slot, TP - 1, 1:1 + WH], src[:, TP - 1], 0, BI_C1_LAST).then_inc(s_o1, 1)
                    return
                if tile:
                    relu(st2[HALF:128, 0, 1:1 + WH], src[HALF:128, TP - 1], HALF)
                relu(o1[:, slot, :, 1:1 + WH], src).then_inc(s_o1, 1)

            def step(i, j):
                odd = j % 2
                b = (j + 3) // 2 if odd else (j + 2) // 2
                gather_perception(i, j + 1, (0, 1))
                if isinstance(i, int) and i == 0 and j == 0:
                    act.wait_ge(s_const, 96)
                    act.wait_ge(s_upd, 2)
                    act.wait_ge(s_zero, 2)
                hidden(i, j, 0)
                hidden(i, j, 1)
                gather_perception(i, j + 1, (2, 3))
                split_hi(i, b, 2 if odd else 1)
                hidden(i, j, 2)
                hidden(i, j, 3)
                if odd:
                    split_hi(i, b, 0)
                conv1_out(i, j - LAG_C1)

            walk(act, step)

        @block.vector
        def _(dve):
            dve.memset(above[:], 0.0).then_inc(s_zero, 1)
            for buf in (o1[:], st2[:]):
                for column in (0, HP - 1):
                    dve.memset(buf[..., column:column + 1], 0.0)
            dve.memset(st0[:], 0.0)
            dve.memset(nb[:], 0.0)
            half = PAIRS // 2
            for n, buf in enumerate((ru0, ru1)):
                dve.wait_ge(s_ru[n], 16)
                dve.tensor_scalar(upd[:, n * half:(n + 1) * half, :].rearrange("p j n -> p (j n)"),
                                  buf[:, 0:half * N], 0.5, None, ALU.is_lt).then_inc(s_upd, 1)
            dve.wait_ge(s_upd, 2)
            dve.memset(x[:, :, :, 0:1], 0.0)
            dve.memset(x[:, :, :, HP - 1:HP], 0.0).then_inc(s_zero, 1)
            dve.wait_ge(s_const, 96)
            dve.tensor_copy(wa_hi[:], wa[:]).then_inc(s_wsplit, 1)
            dve.wait_ge(s_wsplit, 1)
            dve.tensor_tensor(wa_lo[:], wa[:], wa_hi[:].bitcast(f32), ALU.subtract).then_inc(s_wsplit, 1)
            def split_lo(i, b, kind):
                if not there(i, b, NBLOCK, BLOCKS):
                    return
                after(dve, s_hi[kind], i, BLOCKS, b + 1)
                dve.tensor_tensor(part(KINDS + kind, b), source(kind, b), part(kind, b).bitcast(f32),
                                  ALU.subtract).then_inc(s_lo[kind], 1)

            def masked_delta(i, q):
                if not there(i, q):
                    return
                j = q % PAIRS
                after(dve, s_dmm, i, PAIRS, q + 1)
                after(dve, s_x1, i, PAIRS, q)
                dve.scalar_tensor_tensor(out=delta[:], in0=ps_delta[:], scalar=bias[:, BI_DELTA:BI_DELTA + 1],
                                         in1=upd[:, j, :],
                                         op0=ALU.add, op1=ALU.mult).then_inc(s_dev, 1)

            def make_x1(i, q):
                if not there(i, q):
                    return
                after(dve, s_dev, i, PAIRS, q + 1)
                after(dve, s_xl[q // 2 % 2], i, 16 * BLOCKS // 2, 16 * (q // 4 + 1))
                here = x[:, q % XRING, :, 1:1 + WH]
                dve.tensor_tensor(here, here, delta[:].rearrange("p (t w) -> p t w", t=TP), ALU.add).then_inc(s_x1, 1)

            def compare(i, q):
                if not there(i, q):
                    return
                after(dve, s_x1, i, PAIRS, q + 1)
                after(dve, s_aw[q % 2], i, 16 * PAIRS // 2, 16 * (q // 2))
                dve.tensor_scalar(above[:, q % 2].rearrange("p (t w) -> p t w", t=TP), x[:, q % XRING, :, 1:1 + WH],
                                  0.1, None, ALU.is_gt).then_inc(s_above, 1)

            def make_alive(i, q):
                if not there(i, q):
                    return
                rows = nb[:, q % 2]
                after(dve, s_nb[q % 2], i, 16 * PAIRS // 2, 16 * (q // 2 + 1))
                dve.tensor_tensor(m1[:], rows[:, 1, :, 0], rows[:, 1, :, 1], ALU.max).then_inc(s_m1, 1)
                after(dve, s_m1, i, PAIRS, q + 1)
                dve.tensor_tensor(m2[:, :, 0], m1[:], rows[:, 0, :, 1], ALU.max)
                dve.tensor_tensor(m2[:, :, 1], m1[:], rows[:, 2, :, 0], ALU.max).then_inc(s_m2, 1)
                after(dve, s_m2, i, PAIRS, q + 1)
                dve.tensor_tensor(m3[:], m2[:, 0, :, 1:1 + WH], m2[:, 1, :, 1:1 + WH], ALU.max).then_inc(s_m3, 1)
                after(dve, s_m3, i, PAIRS, q + 1)
                after(dve, s_mw, i, 16 * PAIRS, 16 * (q - 1))
                mask = alive[:, q % 2, :].rearrange("p (e l w) -> p e l w", e=2, l=2)
                dve.tensor_tensor(mask[:, 0], m3[:], m2[:, 1, :, 0:WH], ALU.max)
                dve.tensor_tensor(mask[:, 1], m3[:], m2[:, 0, :, 2:HP], ALU.max).then_inc(s_alive, 1)

            def apply_alive(i, q):
                if not there(i, q):
                    return
                j, slot, tile = q % PAIRS, q % XRING, TP * (q % 2)
                after(dve, s_mb[q % 2], i, 16 * PAIRS // 2, 16 * (q // 2 + 1))
                here = x[:, slot, :, 1:1 + WH]
                mask = alive_b[:, q % 2].rearrange("p (t w) -> p t w", t=TP)
                dve.tensor_tensor(here, here, mask, ALU.mult).then_inc(s_x2, 1)
                after(dve, s_x2, i, PAIRS, q + 1)
                after(dve, s_c1, i, PAIRS, q - 1)
                dve.tensor_copy(st1[HALF:128, tile:tile + TP, :], x[HALF:128, slot])
                if tile:
                    dve.tensor_copy(st1[0:HALF, tile - 1:tile - 1 + TP, :], x[0:HALF, slot]).then_inc(s_st1, 1)
                else:
                    dve.tensor_copy(st1[0:HALF, 0:TP - 1, :], x[0:HALF, slot, 1:TP])
                    if j == 0:
                        dve.tensor_copy(st0[0:HALF, :], x[0:HALF, slot, 0]).then_inc(s_st0, 1)
                    else:
                        dve.tensor_copy(st1[0:HALF, 2 * TP - 1, :], x[0:HALF, slot, 0]).then_inc(s_st1, 1)
                if j == PAIRS - 1:
                    dve.memset(st1[0:HALF, tile + TP - 1, :], 0.0).then_inc(s_st1, 1)

            def output(i, q):
                if not there(i, q):
                    return
                after(dve, s_c2, i, PAIRS, q + 1)
                after(dve, s_x2, i, PAIRS, q + 1)
                after(dve, s_out[q // 2 % 2], i, 16 * BLOCKS // 2, 16 * (q // 4))
                dve.scalar_tensor_tensor(out=y[:, q % YRING].rearrange("p (t w) -> p t w", t=TP),
                                         in0=ps_c2[:].rearrange("p (t w) -> p t w", t=TP),
                                         scalar=bias[:, BI_C2:BI_C2 + 1], in1=x[:, q % XRING, :, 1:1 + WH],
                                         op0=ALU.add, op1=ALU.add).then_inc(s_y, 1)

            def step(i, j):
                odd = j % 2
                b = (j + 3) // 2 if odd else (j + 2) // 2
                masked_delta(i, j - LAG_XP)
                make_x1(i, j - LAG_XP)
                compare(i, j - LAG_XP)
                make_alive(i, j - LAG_POOL)
                apply_alive(i, j - LAG_ALIVE)
                split_lo(i, b, 2 if odd else 1)
                output(i, j - LAG_C2)
                if odd:
                    split_lo(i, b, 0)

            walk(dve, step)

        @block.tensor
        def _(pe):
            def hidden(i, q, m):
                if not there(i, q):
                    return
                after(pe, s_perc[q % 2][m], i, 16 * PAIRS // 2, 16 * (q // 2 + 1))
                after(pe, s_hev, i, CHUNKS * PAIRS, CHUNKS * q + m - 1)
                for n in range(2):
                    rhs = perc[:, q % 2, m, 2 * n:2 * n + 2].rearrange("k r e w -> k (r e w)")
                    out = ps_hid[m % 2][:, n, :]
                    nc.tensor.matmul(out, wa_hi[:], rhs, start=True, stop=False)
                    last = nc.tensor.matmul(out, wa_lo[:], rhs, start=False, stop=True)
                last.then_inc(s_hmm, 1)

            def delta_products(i, q):
                if not there(i, q):
                    return
                after(pe, s_hev, i, CHUNKS * PAIRS, CHUNKS * (q + 1))
                after(pe, s_dev, i, PAIRS, q)
                for n in range(2):
                    for t in range(4):
                        row = 2 * (t // 2) + n
                        last = nc.tensor.matmul(ps_delta[32 * t:32 * t + 32, :], w2[:, n, :], hid[:, 2 * row + t % 2, :],
                                                start=(n == 0), stop=(n == 1))
                last.then_inc(s_dmm, 1)

            def product(out, weights, source, e, shift, columns=slice(0, N)):
                return nc.tensor.matmul(out[0][32 * out[1]:32 * out[1] + 32, columns], weights[:, e, shift, :],
                                        source[:, :, e + shift:e + shift + WH],
                                        start=(shift == 0), stop=(shift == 1), tile_position=(0, 32 * out[1]))

            def conv1(i, q):
                if not there(i, q):
                    return
                j, slot = q % PAIRS, q % XRING
                after(pe, s_x2, i, PAIRS, q + 1)
                after(pe, s_o1, i, PAIRS, q)
                if j == 0:
                    after(pe, s_st0, i, 1, q // PAIRS + 1)
                    after(pe, s_topev, i, 1, q // PAIRS)
                    for shift in range(2):
                        for e in range(2):
                            last = product((ps_top, 2 + e), g1v[:, 0], st0[:].unsqueeze(1), e, shift, slice(0, WH))
                    last.then_inc(s_top, 1)
                tile = TP * (q % 2)
                split = j == PAIRS - 1
                for shift in range(2):
                    for e in range(2):
                        last = product((ps_c1, e), g1[:, 0], x[:, slot], e, shift)
                    if shift == 0:
                        after(pe, s_st1, i, PAIRS, q + 1)
                    if not split:
                        for e in range(2):
                            last = product((ps_c1, 2 + e), g1[:, 1], st1[:, tile:tile + TP], e, shift)
                if split:
                    for weights, a, b in ((g1[:, 1], 0, TP - 1), (g1v[:, 1], TP - 1, TP)):
                        for shift in range(2):
                            for e in range(2):
                                last = product((ps_c1, 2 + e), weights, st1[:, tile + a:tile + b], e, shift,
                                               slice(a * WH, b * WH))
                last.then_inc(s_c1, 1)

            def conv2(i, q, shift):
                if not there(i, q):
                    return
                tile = TP * (q % 2)
                if shift == 0:
                    after(pe, s_o1, i, PAIRS, q + 1)
                    after(pe, s_y, i, PAIRS, q)
                for e in range(2):
                    product((ps_c2, e), g2[:, 1], st2[:, tile:tile + TP], e, shift)
                for e in range(2):
                    last = product((ps_c2, 2 + e), g2[:, 0], o1[:, q % ORING], e, shift)
                if shift == 1:
                    last.then_inc(s_c2, 1)

            def step(i, j):
                hidden(i, j, 0)
                hidden(i, j, 1)
                conv2(i, j - LAG_C2, 0)
                hidden(i, j, 2)
                hidden(i, j, 3)
                conv2(i, j - LAG_C2, 1)
                conv1(i, j - LAG_C1)
                delta_products(i, j)

            pe.wait_ge(s_const, 96)
            pe.wait_ge(s_wsplit, 2)
            pe.wait_ge(s_zero, 2)
            walk(pe, step)


def band(w, straddle, rows=(0, 1)):
    out = np.zeros((2, 2, 2, C, 2, 2, 2, C), w.dtype)
    for rh in range(2):
        for rl in range(2):
            place = 2 * (1 - rh if straddle else rh) + rl
            for s in range(2):
                for e in range(2):
                    for shift in range(2):
                        dx = s + 2 * shift + e - 1
                        for r in rows:
                            if 0 <= place - r <= 2 and 0 <= dx <= 2:
                                out[rh, s, rl, :, e, shift, r] = w[:, :, place - r, dx].T
    return out.reshape(128, 2, 2, 2 * C)


def kernel(x, L0_conv_rand_u, L0_conv_W1, L0_conv_b1, L0_conv_W2, L0_conv_b2,
           L1_conv_w1, L1_conv_b1, L1_conv_w2, L1_conv_b2):
    import concourse.bacc as bacc
    from concourse.bass_utils import run_bass_kernel_spmd

    x = np.asarray(x)
    padded = np.zeros((B, C, H + 2, WP), x.dtype)
    padded[:, :, 1:-1, 1:-1] = x
    strips = np.lib.stride_tricks.sliding_window_view(padded, STRIP + 2, axis=2)[:, :, ::STRIP]
    strips = strips.reshape(B, C, BLOCKS, 8, WP, STRIP + 2).transpose(0, 2, 3, 1, 5, 4)
    xs = np.ascontiguousarray(strips).reshape(NBLOCK, 128, (STRIP + 2) * WP)
    xl = x.reshape(B, C, BLOCKS, 2, TP, 2, 2, WH, 2).transpose(0, 2, 5, 8, 6, 1, 3, 4, 7)
    xl = np.ascontiguousarray(xl).reshape(NBLOCK, 128, 2 * N)
    ru = np.asarray(L0_conv_rand_u).reshape(PAIRS, TP, 2, 2, WH, 2).transpose(2, 5, 3, 0, 1, 4)
    ru = np.ascontiguousarray(ru).reshape(GROUPS, PAIRS * N)

    w1 = np.asarray(L0_conv_W1)
    wa = np.zeros((C, PARTS, HID), w1.dtype)
    for part in range(PARTS):
        kind = part % KINDS
        wa[:, part] = w1[:, kind * C:(kind + 1) * C].T
    wa = wa.reshape(KROWS, HID)
    w2t = np.asarray(L0_conv_W2).T
    w2 = np.zeros((HID, 2, 32), w2t.dtype)
    w2[:, 0, :C] = w2t
    w2[:, 1, C:] = w2t
    c1, c2 = np.asarray(L1_conv_w1), np.asarray(L1_conv_w2)
    g1 = np.stack([band(c1, False), band(c1, True)], axis=1)
    g2 = np.stack([band(c2, False), band(c2, True)], axis=1)
    g1v = np.stack([band(c1, True, (1,)), band(c1, True, (0,))], axis=1)

    bias = np.zeros((128, 6), x.dtype)
    bias[:, BI_HID] = np.asarray(L0_conv_b1)
    bias[:, BI_DELTA] = np.tile(np.asarray(L0_conv_b2), 8)
    for col in (BI_C1, BI_C1_TOP, BI_C1_LAST):
        bias[:, col] = np.tile(np.asarray(L1_conv_b1), 8)
    for e in range(2):
        first = HALF + 32 * e
        bias[first:first + C, BI_C1_TOP] = 0
        bias[first + C:first + 2 * C, BI_C1_LAST] = 0
    bias[:, BI_C2] = np.tile(np.asarray(L1_conv_b2), 8)

    nc = bacc.Bacc("TRN2", target_bir_lowering=False, num_devices=1)
    arrays = {"in_xs": xs, "in_xl": xl, "in_ru": ru, "in_wa": wa, "in_w2": w2, "in_g1": g1, "in_g1v": g1v,
              "in_g2": g2, "in_bias": bias}
    args = [nc.dram_tensor(name, a.shape, mybir.dt.from_np(a.dtype), kind="ExternalInput").ap()
            for name, a in arrays.items()]
    out = nc.dram_tensor("out", (NBLOCK, 128, 2 * N), mybir.dt.float32, kind="ExternalOutput").ap()
    build_program(nc, *args, out)
    got = run_bass_kernel_spmd(nc, [arrays], core_ids=[0]).results[0]["out"]
    got = got.reshape(B, BLOCKS, 2, 2, 2, C, 2, TP, WH).transpose(0, 5, 1, 6, 7, 2, 4, 8, 3)
    return np.ascontiguousarray(got).reshape(B, C, H, W)
```
